# Optimizing a Trainium2 kernel written in Bass

```python
import numpy as np
import jax
import jax.numpy as jnp

def _softmax(x, axis=-1):
    return jax.nn.softmax(x, axis=axis)
def _gelu(x):
    return jax.nn.gelu(x, approximate=True)
def _silu(x):
    return jax.nn.silu(x)
def _sigmoid(x):
    return jax.nn.sigmoid(x)
def _layernorm(x, axis=-1, eps=1e-5):
    m = jnp.mean(x, axis=axis, keepdims=True)
    v = jnp.var(x, axis=axis, keepdims=True)
    return (x - m) / jnp.sqrt(v + eps)
def _scatter_add(tgt, idx, src, axis=0):
    return tgt.at[idx].add(src)
def _segment_sum(src, seg, n):
    return jax.ops.segment_sum(src, seg, n)

kernel_name = 'mk_adj_resnorm_d4_adj_512_d500e2'

def setup_inputs(seed: int = 0):
    np.random.seed(seed)
    _w = jnp.asarray
    def _rec_inputs():
        import jax
        import jax.numpy as jnp
        _gk = jax.random.key(seed)
        x = -0.0005207 + 1.001 * jax.random.normal(jax.random.fold_in(_gk, 1), (2708, 512), jnp.float32)
        _w = (1.0 + jnp.arange(2708, dtype=jnp.float32)) ** -0.5
        _w = _w / _w.mean()
        _pij = jnp.clip(0.00590842 * _w[:, None] * _w[None, :], 0.0, 1.0)
        _a = jax.random.uniform(jax.random.fold_in(_gk, 2), (2708, 2708)) < _pij
        _a = jnp.logical_or(_a, jnp.swapaxes(_a, -1, -2))
        _a = jnp.logical_or(_a, jnp.eye(2708, dtype=bool))
        _af = _a.astype(jnp.float32)
        _af = _af * jax.random.uniform(jax.random.fold_in(_gk, 3), (2708, 2708), jnp.float32, 0.05, 5.41998)
        adj = _af
        return x, adj
    x, adj = _rec_inputs()
    def _L0_gnn_setup():
        import jax, jax.numpy as jnp
        import numpy as np
        N, DIN, F, H = (4096, 512, 64, 8)
        EPS = float(np.finfo(np.float64).eps)
        key = jax.random.key(seed)
        ks = jax.random.split(key, 6)
        scale_k = (6.0 / (DIN + F)) ** 0.5
        scale_a = (6.0 / (F + 1)) ** 0.5
        return {'x': jax.random.normal(ks[0], (N, DIN), jnp.float32), 'adj': jax.random.normal(ks[1], (N, N), jnp.float32), 'kernels': jax.random.uniform(ks[2], (H, DIN, F), jnp.float32, -scale_k, scale_k), 'attn_self': jax.random.uniform(ks[3], (H, F), jnp.float32, -scale_a, scale_a), 'attn_neigh': jax.random.uniform(ks[4], (H, F), jnp.float32, -scale_a, scale_a), 'biases': jnp.zeros((H, F), jnp.float32)}
    _L0_gnn_all = _L0_gnn_setup()
    _L0_gnn_in = {k: v for k, v in _L0_gnn_all.items() if k in ('kernels', 'attn_self', 'attn_neigh', 'biases', )}
    del _L0_gnn_all

    def _L1_gnn_setup():
        import jax, jax.numpy as jnp
        import numpy as np
        N = 8192
        D_IN = 512
        HEADS = 8
        DPH = 512 // HEADS
        EDGE_P = 0.01
        key = jax.random.key(seed)
        k1, k2, k3 = jax.random.split(key, 3)
        H = jax.random.normal(k1, (N, D_IN), dtype=jnp.float32)
        adj = (jax.random.uniform(k2, (N, N)) < EDGE_P).astype(jnp.float32)
        limit = float(np.sqrt(6.0 / (D_IN + DPH)))
        W = jax.random.uniform(k3, (HEADS, D_IN, DPH), jnp.float32, -limit, limit)
        b = jnp.zeros((HEADS, DPH), jnp.float32)
        return {'H': H, 'adj': adj, 'W': W, 'b': b}
    _L1_gnn_all = _L1_gnn_setup()
    _L1_gnn_in = {k: v for k, v in _L1_gnn_all.items() if k in ('W', 'b', )}
    del _L1_gnn_all

    def _L2_gnn_setup():
        import jax, jax.numpy as jnp
        import numpy as np
        IN_C, HID_C = (512, 512)
        ALPHA = 0.2
        N = 8192
        NEG_BIG = -9000000000000000.0
        key = jax.random.key(seed)
        k1, k2, k3, k4, k5, k6, k7 = jax.random.split(key, 7)
        h = jax.random.normal(k1, (N, IN_C), dtype=jnp.float32)
        adj = jax.random.randint(k2, (N, N), 0, 2).astype(jnp.float32)
        gain = np.sqrt(2.0 / (1.0 + ALPHA ** 2))
        lim_W = gain * np.sqrt(6.0 / (2 * IN_C + HID_C))
        W = jax.random.uniform(k3, (2 * IN_C, HID_C), jnp.float32, -lim_W, lim_W)
        lim_a = np.sqrt(1.0 / HID_C)
        a_w = jax.random.uniform(k4, (HID_C,), jnp.float32, -lim_a, lim_a)
        a_b = jax.random.uniform(k5, (), jnp.float32, -lim_a, lim_a)
        lim_fc = np.sqrt(1.0 / IN_C)
        fc_w = jax.random.uniform(k6, (IN_C, HID_C), jnp.float32, -lim_fc, lim_fc)
        fc_b = jax.random.uniform(k7, (HID_C,), jnp.float32, -lim_fc, lim_fc)
        return {'h': h, 'adj': adj, 'W': W, 'a_w': a_w, 'a_b': a_b, 'fc_w': fc_w, 'fc_b': fc_b}
    _L2_gnn_all = _L2_gnn_setup()
    _L2_gnn_in = {k: v for k, v in _L2_gnn_all.items() if k in ('W', 'a_w', 'a_b', 'fc_w', 'fc_b', )}
    del _L2_gnn_all

    def _L3_gnn_setup():
        import jax, jax.numpy as jnp
        import numpy as np
        N, F, H = (3072, 512, 4)
        D = F // H
        ALPHA = 0.5
        EPS = 1e-06

        def _batchnorm(x, gamma, beta):
            m = jnp.mean(x, axis=0)
            v = jnp.var(x, axis=0)
            return (x - m) * jax.lax.rsqrt(v + EPS) * gamma + beta

        def _masked_softmax(scores, mask):
            s = jnp.where(mask, scores, -jnp.inf)
            att = jax.nn.softmax(s, axis=-1)
            return jnp.where(mask, att, 0.0)

        def _mlp_block(x, Wm, bm, g, b):
            h = jax.nn.elu(x @ Wm.T + bm) + x
            return _batchnorm(h, g, b)
        key = jax.random.key(seed)
        ks = jax.random.split(key, 12)
        X = jax.random.normal(ks[0], (N, F), dtype=jnp.float32)
        eye = jnp.eye(N, dtype=jnp.float32)
        local = (jax.random.uniform(ks[1], (N, N)) < 32.0 / N).astype(jnp.float32)
        local = jnp.clip(local + eye, 0.0, 1.0)
        longr = (jax.random.uniform(ks[2], (N, N)) < 16.0 / N).astype(jnp.float32)
        longr = jnp.clip(longr + eye, 0.0, 1.0)
        W = jax.random.normal(ks[3], (H, D, D), dtype=jnp.float32) * 0.1
        V = jax.random.normal(ks[4], (H, 2, D, 1), dtype=jnp.float32) * 0.1
        return {'X': X, 'local_pattern': local, 'long_range_pattern': longr, 'W': W, 'V': V, 'enc_bn_gamma': jnp.ones((F,), jnp.float32), 'enc_bn_beta': jnp.zeros((F,), jnp.float32), 'enc_mlp_W': jax.random.normal(ks[5], (F, F), dtype=jnp.float32) * 0.02, 'enc_mlp_b': jnp.zeros((F,), jnp.float32), 'enc_mlp_bn_gamma': jnp.ones((F,), jnp.float32), 'enc_mlp_bn_beta': jnp.zeros((F,), jnp.float32), 'dec_mlp_W': jax.random.normal(ks[6], (F, F), dtype=jnp.float32) * 0.02, 'dec_mlp_b': jnp.zeros((F,), jnp.float32), 'dec_mlp_bn_gamma': jnp.ones((F,), jnp.float32), 'dec_mlp_bn_beta': jnp.zeros((F,), jnp.float32)}
    _L3_gnn_all = _L3_gnn_setup()
    _L3_gnn_in = {k: v for k, v in _L3_gnn_all.items() if k in ('W', 'V', 'enc_bn_gamma', 'enc_bn_beta', 'enc_mlp_W', 'enc_mlp_b', 'enc_mlp_bn_gamma', 'enc_mlp_bn_beta', 'dec_mlp_W', 'dec_mlp_b', 'dec_mlp_bn_gamma', 'dec_mlp_bn_beta', )}
    del _L3_gnn_all

    return {
        "x": x,
        "adj": adj,
        "L0_gnn_kernels": _L0_gnn_in["kernels"],
        "L0_gnn_attn_self": _L0_gnn_in["attn_self"],
        "L0_gnn_attn_neigh": _L0_gnn_in["attn_neigh"],
        "L0_gnn_biases": _L0_gnn_in["biases"],
        "L1_gnn_W": _L1_gnn_in["W"],
        "L1_gnn_b": _L1_gnn_in["b"],
        "L2_gnn_W": _L2_gnn_in["W"],
        "L2_gnn_a_w": _L2_gnn_in["a_w"],
        "L2_gnn_a_b": _L2_gnn_in["a_b"],
        "L2_gnn_fc_w": _L2_gnn_in["fc_w"],
        "L2_gnn_fc_b": _L2_gnn_in["fc_b"],
        "L3_gnn_W": _L3_gnn_in["W"],
        "L3_gnn_V": _L3_gnn_in["V"],
        "L3_gnn_enc_bn_gamma": _L3_gnn_in["enc_bn_gamma"],
        "L3_gnn_enc_bn_beta": _L3_gnn_in["enc_bn_beta"],
        "L3_gnn_enc_mlp_W": _L3_gnn_in["enc_mlp_W"],
        "L3_gnn_enc_mlp_b": _L3_gnn_in["enc_mlp_b"],
        "L3_gnn_enc_mlp_bn_gamma": _L3_gnn_in["enc_mlp_bn_gamma"],
        "L3_gnn_enc_mlp_bn_beta": _L3_gnn_in["enc_mlp_bn_beta"],
        "L3_gnn_dec_mlp_W": _L3_gnn_in["dec_mlp_W"],
        "L3_gnn_dec_mlp_b": _L3_gnn_in["dec_mlp_b"],
        "L3_gnn_dec_mlp_bn_gamma": _L3_gnn_in["dec_mlp_bn_gamma"],
        "L3_gnn_dec_mlp_bn_beta": _L3_gnn_in["dec_mlp_bn_beta"],
    }

def reference(x, adj, L0_gnn_kernels, L0_gnn_attn_self, L0_gnn_attn_neigh, L0_gnn_biases, L1_gnn_W, L1_gnn_b, L2_gnn_W, L2_gnn_a_w, L2_gnn_a_b, L2_gnn_fc_w, L2_gnn_fc_b, L3_gnn_W, L3_gnn_V, L3_gnn_enc_bn_gamma, L3_gnn_enc_bn_beta, L3_gnn_enc_mlp_W, L3_gnn_enc_mlp_b, L3_gnn_enc_mlp_bn_gamma, L3_gnn_enc_mlp_bn_beta, L3_gnn_dec_mlp_W, L3_gnn_dec_mlp_b, L3_gnn_dec_mlp_bn_gamma, L3_gnn_dec_mlp_bn_beta):
    import jax
    import jax.numpy as jnp
    def _L0_gnn_ref(x, adj, kernels, attn_self, attn_neigh, biases):
        import jax, jax.numpy as jnp
        import numpy as np
        N, DIN, F, H = (4096, 512, 64, 8)
        EPS = float(np.finfo(np.float64).eps)
        mask = (adj > 0).astype(x.dtype)
        outs = []
        for h in range(kernels.shape[0]):
            feats = x @ kernels[h]
            a_s = feats @ attn_self[h]
            a_n = feats @ attn_neigh[h]
            diff = a_s[:, None] - a_n[None, :]
            dense = jnp.exp(-(diff * diff)) * mask
            dense = dense / (dense.sum(axis=1, keepdims=True) + EPS)
            outs.append(dense @ feats + biases[h])
        out = jnp.concatenate(outs, axis=-1)
        return jax.nn.relu(out)

    def _L1_gnn_ref(H, adj, W, b):
        import jax, jax.numpy as jnp
        import numpy as np
        N = 8192
        D_IN = 512
        HEADS = 8
        DPH = 512 // HEADS
        EDGE_P = 0.01
        H_ = jnp.einsum('nd,hde->hne', H, W)
        out = jnp.einsum('nm,hme->hne', adj, H_) + b[:, None, :]
        return jnp.transpose(out, (1, 0, 2)).reshape(H.shape[0], HEADS * DPH)

    def _L2_gnn_ref(h, adj, W, a_w, a_b, fc_w, fc_b):
        import jax, jax.numpy as jnp
        import numpy as np
        IN_C, HID_C = (512, 512)
        ALPHA = 0.2
        N = 8192
        NEG_BIG = -9000000000000000.0
        Wh1 = h @ W[:IN_C]
        Wh2 = h @ W[IN_C:]
        s1 = Wh1 @ a_w
        s2 = Wh2 @ a_w
        e = s1[:, None] + s2[None, :] + a_b
        e = jnp.where(e >= 0, e, ALPHA * e)
        e = jnp.where(adj > 0, e, NEG_BIG)
        att = jax.nn.softmax(e, axis=1)
        return att @ (h @ fc_w + fc_b)

    def _L3_gnn_ref(X, local_pattern, long_range_pattern, W, V, enc_bn_gamma, enc_bn_beta, enc_mlp_W, enc_mlp_b, enc_mlp_bn_gamma, enc_mlp_bn_beta, dec_mlp_W, dec_mlp_b, dec_mlp_bn_gamma, dec_mlp_bn_beta):
        import jax, jax.numpy as jnp
        import numpy as np
        N, F, H = (3072, 512, 4)
        D = F // H
        ALPHA = 0.5
        EPS = 1e-06

        def _batchnorm(x, gamma, beta):
            m = jnp.mean(x, axis=0)
            v = jnp.var(x, axis=0)
            return (x - m) * jax.lax.rsqrt(v + EPS) * gamma + beta

        def _masked_softmax(scores, mask):
            s = jnp.where(mask, scores, -jnp.inf)
            att = jax.nn.softmax(s, axis=-1)
            return jnp.where(mask, att, 0.0)

        def _mlp_block(x, Wm, bm, g, b):
            h = jax.nn.elu(x @ Wm.T + bm) + x
            return _batchnorm(h, g, b)
        n = X.shape[0]
        Xh = X.reshape(n, H, D).transpose(1, 0, 2)
        Xw = jnp.einsum('hnd,hde->hne', Xh, W)
        f1 = jnp.einsum('hnd,hd->hn', Xw, V[:, 0, :, 0])
        f2 = jnp.einsum('hnd,hd->hn', Xw, V[:, 1, :, 0])
        sig = jax.nn.sigmoid(f1[:, :, None] + f2[:, None, :])
        lmask = (local_pattern != 0)[None]
        gmask = (long_range_pattern != 0)[None]
        local_att = _masked_softmax(local_pattern[None] * sig, lmask)
        long_att = _masked_softmax(long_range_pattern[None] * sig, gmask)
        att = ALPHA * long_att + (1.0 - ALPHA) * local_att
        Xa = jnp.einsum('hij,hjd->hid', att, Xw)
        Xc = Xa.transpose(1, 0, 2).reshape(n, F)
        Xn = _batchnorm(Xc, enc_bn_gamma, enc_bn_beta)
        emb = _mlp_block(Xn, enc_mlp_W, enc_mlp_b, enc_mlp_bn_gamma, enc_mlp_bn_beta)
        Yh = emb.reshape(n, H, D).transpose(1, 0, 2)
        Y = jnp.einsum('hij,hjd->hid', att, Yh)
        Y = jnp.einsum('hnd,hed->hne', Y, W)
        Yc = Y.transpose(1, 0, 2).reshape(n, F)
        Yc = jax.nn.elu(Yc)
        out = _mlp_block(Yc, dec_mlp_W, dec_mlp_b, dec_mlp_bn_gamma, dec_mlp_bn_beta)
        return out

    x = _layernorm(x + _L0_gnn_ref(x, adj, L0_gnn_kernels, L0_gnn_attn_self, L0_gnn_attn_neigh, L0_gnn_biases), axis=-1)
    x = _layernorm(x + _L1_gnn_ref(x, adj, L1_gnn_W, L1_gnn_b), axis=-1)
    x = _layernorm(x + _L2_gnn_ref(x, adj, L2_gnn_W, L2_gnn_a_w, L2_gnn_a_b, L2_gnn_fc_w, L2_gnn_fc_b), axis=-1)
    x = _layernorm(x + _L3_gnn_ref(x, adj, adj, L3_gnn_W, L3_gnn_V, L3_gnn_enc_bn_gamma, L3_gnn_enc_bn_beta, L3_gnn_enc_mlp_W, L3_gnn_enc_mlp_b, L3_gnn_enc_mlp_bn_gamma, L3_gnn_enc_mlp_bn_beta, L3_gnn_dec_mlp_W, L3_gnn_dec_mlp_b, L3_gnn_dec_mlp_bn_gamma, L3_gnn_dec_mlp_bn_beta), axis=-1)
    return x


_drawn_inputs = setup_inputs


def setup_inputs(seed=0):
    import zlib

    import numpy as np

    out = dict(_drawn_inputs(seed))
    spreads = {'L0_gnn_biases': (0.0, 0.1),
     'L1_gnn_b': (0.0, 0.8),
     'L3_gnn_enc_bn_gamma': (1.0, 0.2),
     'L3_gnn_enc_bn_beta': (0.0, 2.0),
     'L3_gnn_enc_mlp_b': (0.0, 0.8),
     'L3_gnn_enc_mlp_bn_gamma': (1.0, 0.2),
     'L3_gnn_enc_mlp_bn_beta': (0.0, 0.336),
     'L3_gnn_dec_mlp_b': (0.0, 0.646),
     'L3_gnn_dec_mlp_bn_gamma': (1.0, 0.2),
     'L3_gnn_dec_mlp_bn_beta': (0.0, 0.1)}
    factors = {'L2_gnn_fc_b': 2.922}
    for name, (base, spread) in spreads.items():
        noise = np.random.default_rng([zlib.crc32(name.encode()), seed]).standard_normal(out[name].shape)
        drawn = base * np.exp(spread * noise) if base else spread * noise
        out[name] = jnp.asarray(drawn.astype(out[name].dtype))
    for name, factor in factors.items():
        out[name] = (out[name] * factor).astype(out[name].dtype)
    return out
```

```python
import concourse.bass as bass
from concourse import mybir
from contextlib import ExitStack

FP32 = mybir.dt.float32
U8 = mybir.dt.uint8
ALU = mybir.AluOpType
ACT = mybir.ActivationFunctionType
AX = mybir.AxisListType

N = 2708
D = 512
T = 22
P = 124
NP = T * P
TAIL = N - (T - 1) * P
PAIRS = T // 2
KT = D // 128
H0, F0 = 8, 64
FW = F0 + 1
H3, D3 = 4, 128
CH = 2
CT = T // CH
CW = CT * P
TA = 6
GROUPS = [(a, min(a + 4, T)) for a in range(0, T, 4)]
NG = len(GROUPS)
EPS0 = 2.220446049250313e-16
LN_EPS = 1e-5
BN_EPS = 1e-6
FAR = 255.0
NEG = -9e15
LOW = -3e38
SQ_ON_ACT = [m % 5 in (0, 2, 4) for m in range(T)]


def wait(eng, sem, value):
    if isinstance(value, int) and value <= 0:
        return
    eng.wait_ge(sem, value)


def count(eng, value):
    return value if isinstance(value, int) else eng.to_reg(value)


def carry(eng, settled, value):
    eng.wait_ge(settled, value)


def pair_loop(eng, body, first=0, last=False):
    lo, hi = int(first), PAIRS - int(last)
    for i in range(lo):
        body(i)
    with eng.Fori(lo, hi) as i:
        body(i)
    if last:
        body(PAIRS - 1)


def build(nc, x, adj_rows, adj_cols, adj_tiles, ident, w0, a0_self, a0_neigh, b0, w1, b1, w2a, w2b, a2_w, a2_b,
          fc_w, fc_b, w3, w3t, v3a, v3b, enc_w, enc_b, dec_w, dec_b, g_bn, b_bn, out, dbg=None):
    top = ExitStack()
    kind = "ExternalOutput" if dbg else "Internal"

    def scratch(name, shape):
        return nc.dram_tensor(name, shape, FP32, kind=kind).ap()

    xs = [scratch(f"x_after_{k}", [T, P, D]) for k in range(3)]
    rows0 = scratch("score_rows_0", [H0, NP])
    rows2 = scratch("score_rows_2", [1, NP])
    rows3 = scratch("score_rows_3", [H3, NP])
    xc_dram = scratch("attended", [T, P, D])
    h2_dram = scratch("decoded", [T, P, D])

    def sem(name):
        return top.enter_context(nc.semaphore(name))

    def sems(name, n=2):
        return [sem(f"{name}{k}") for k in range(n)]

    names = set()

    def sb(stack, name, shape, dt=FP32):
        k = 0
        while f"{name}_{k}" in names:
            k += 1
        names.add(f"{name}_{k}")
        return stack.enter_context(nc.sbuf_tensor(f"{name}_{k}", shape, dt))

    with top:
        HA = sb(top, "HA", [128, T, H0 * FW])
        idt = sb(top, "idt", [128, 128])
        ones = sb(top, "ones", [128, 128])
        u0s, u0n = sb(top, "u0s", [128, KT, H0]), sb(top, "u0n", [128, KT, H0])
        u2s, u2n = sb(top, "u2s", [128, KT, 1]), sb(top, "u2n", [128, KT, 1])
        u3s, u3n = sb(top, "u3s", [128, KT, H3]), sb(top, "u3n", [128, KT, H3])
        neg_t = sb(top, "neg_t", [128, T, H0])
        s1 = sb(top, "s1", [128, T])
        f1 = sb(top, "f1", [128, T, H3])
        half = sb(top, "half", [128, 1])
        ab2 = sb(top, "ab2", [128, 1])
        bank = [top.enter_context(nc.psum_tensor(f"bank{k}", [128, 512], FP32)) for k in range(8)]
        acc = bank[0:2]
        turn = bank[2:5]
        etp, pj, sc = bank[5], bank[6], bank[7]

        set_const = sem("set_const")
        turned, turned_out = sem("turned"), sem("turned_out")
        proj_mm, proj_out = sem("proj_mm"), sem("proj_out")
        score_mm, score_out = sem("score_mm"), sem("score_out")
        x_in = sems("x_in")
        r_half, r_full = sem("r_half"), sem("r_full")
        ln_stats, ln_mean, ln_var, ln_rstd, ln_done = (sem(f"ln_{k}") for k in ("stats", "mean", "var", "rstd", "done"))
        xn_stored = sems("xn_stored")
        row_stored = sems("row_stored")

        def etp_view(n=P):
            return etp[:, 0:KT * n].rearrange("p (k n) -> p k n", k=KT)

        def turn_tile(pe, n, src):
            wait(pe, turned_out, n)
            for k in range(KT):
                t = pe.transpose(etp_view()[:, k, :], src[0:P, k * 128:(k + 1) * 128], idt[0:P, 0:P])
            t.then_inc(turned, 1)

        def keep_turned(act, n, xt):
            act.wait_ge(turned, n + 1)
            wait(act, proj_mm, n - 1)
            act.activation(xt[:, :, :], etp_view(), ACT.Copy).then_inc(turned_out, 1)

        def project(pe, n, xt, w, u_col, u_row, heads, blocked=False):
            pe.wait_ge(turned_out, n + 1)
            if heads:
                wait(pe, score_out, score_base[0] + n)
                for k in range(KT):
                    pe.matmul(sc[0:P, 0:heads], xt[:, k, :], u_col[:, k, :], start=(k == 0), stop=(k == KT - 1))
                for k in range(KT):
                    t = pe.matmul(sc[0:heads, 16:16 + P], u_row[:, k, :], xt[:, k, :],
                                  start=(k == 0), stop=(k == KT - 1))
                t.then_inc(score_mm, 1)
            wait(pe, proj_out, n)
            for k in range(KT):
                if blocked:
                    t = pe.matmul(pj[0:P, k * D3:(k + 1) * D3], xt[:, k, :], w[:, k, :], start=True, stop=True)
                else:
                    t = pe.matmul(pj[0:P, :], xt[:, k, :], w[:, k, :], start=(k == 0), stop=(k == KT - 1))
            t.then_inc(proj_mm, 1)

        score_base = [0]

        def ln_tile(dve, n, q, R, st, xn):
            dve.wait_ge(r_full, n + 1)
            dve.bn_stats(st[q][:, 0:6], R[q][:, :]).then_inc(ln_stats, 1)
            carry(dve, set_const, 1)
            dve.wait_ge(ln_stats, n + 1)
            dve.bn_aggr(st[q][:, 6:8], st[q][:, 0:6]).then_inc(ln_mean, 1)
            dve.wait_ge(ln_mean, n + 1)
            dve.tensor_scalar(st[q][:, 8:9], st[q][:, 7:8], LN_EPS, None, ALU.add).then_inc(ln_var, 1)
            dve.wait_ge(ln_rstd, n + 1)

        def ln_write(dve, n, q, R, st, dst):
            dve.tensor_scalar(dst, R[q][:, :], st[q][:, 6:7], st[q][:, 9:10], ALU.subtract, ALU.mult)\
               .then_inc(ln_done, 1)

        def ln_power(pool, n, q, st):
            pool.wait_ge(ln_var, n + 1)
            pool.tensor_tensor(st[q][:, 9:10], st[q][:, 8:9], half[0:P, :], ALU.pow).then_inc(ln_rstd, 1)

        L0 = ExitStack()
        HB = sb(L0, "HB", [128, T, D])
        with ExitStack() as ph:
            msk_stack = ExitStack()
            msk = sb(msk_stack, "msk", [P, T, NP], U8)
            w0_sb = sb(ph, "w0_sb", [128, KT, D])
            xin = [sb(ph, f"xin{q}", [P, D]) for q in (0, 1)]
            xt = [sb(ph, f"xt{q}", [128, KT, P]) for q in (0, 1)]
            srow = [sb(ph, f"srow{q}", [H0, P]) for q in (0, 1)]
            al = [sb(ph, f"al{q}", [P, NP]) for q in (0, 1)]
            vec = HB[:, 16:18, :]
            tmp = HB[:, 0:4, :]
            wld = HB[:, 4:16, :]
            w_in, vec_in, u_in = sem("w0_in"), sem("vec0_in"), sem("fold_in")
            adj_in, mask_done = sems("mask_adj_in"), sem("mask_done")
            fold_mul, fold_sum = sem("fold_mul"), sem("fold_sum")
            vecs = [HB[:, 16 + k, :] for k in range(5)]
            with nc.Block() as block:
                @block.sync
                def _(sp):
                    sp.dma_start(w0_sb[:, :, :], w0).then_inc(w_in, 16)
                    sp.dma_start(vecs[0], a0_self.partition_broadcast(128)).then_inc(vec_in, 16)
                    sp.dma_start(vecs[1], a0_neigh.partition_broadcast(128)).then_inc(vec_in, 16)
                    sp.dma_start(idt[:, :], ident).then_inc(vec_in, 16)

                    def body(i):
                        for q in (0, 1):
                            j = 2 * i + q
                            wait(sp, turned, j - 1)
                            sp.dma_start(xin[q][:, :], x[j]).then_inc(x_in[q], 16)
                            wait(sp, mask_done, j - 1)
                            sp.dma_start(al[q][:, :], adj_cols[j]).then_inc(adj_in[q], 16)
                    pair_loop(sp, body, first=True)

                @block.gpsimd
                def _(pool):
                    pool.dma_start(vecs[2], a2_w.partition_broadcast(128)).then_inc(u_in, 16)
                    pool.dma_start(vecs[3], v3a.partition_broadcast(128)).then_inc(u_in, 16)
                    pool.dma_start(vecs[4], v3b.partition_broadcast(128)).then_inc(u_in, 16)
                    pool.dma_start(wld[:, 0:4, :], w2a).then_inc(u_in, 16)
                    pool.dma_start(wld[:, 4:8, :], w2b).then_inc(u_in, 16)
                    pool.dma_start(wld[:, 8, :], w3).then_inc(u_in, 16)
                    pool.dma_start(ab2[:, :], a2_b.partition_broadcast(128)).then_inc(u_in, 16)

                    def body(i):
                        for q in (0, 1):
                            pool.wait_ge(score_out, 2 * (2 * i + q) + 2)
                            pool.dma_start(rows0[:, bass.ds((2 * i + q) * P, P)], srow[q][:, :])\
                                .then_inc(row_stored[q], 16)
                    pair_loop(pool, body)
                    for q in (0, 1):
                        pool.wait_ge(row_stored[q], 16 * PAIRS)
                    pool.wait_ge(u_in, 7 * 16)

                @block.tensor
                def _(pe):
                    pe.wait_ge(vec_in, 48)
                    pe.wait_ge(w_in, 16)

                    def scores(n, q):
                        pe.wait_ge(turned_out, n + 1)
                        wait(pe, score_out, 2 * n)
                        if isinstance(n, int) and n == 0:
                            pe.wait_ge(fold_sum, 2)
                        for k in range(KT):
                            pe.matmul(sc[0:P, 0:H0], xt[q][:, k, :], u0n[:, k, :], start=(k == 0), stop=(k == KT - 1))
                        for k in range(KT):
                            t = pe.matmul(sc[0:H0, 16:16 + P], u0s[:, k, :], xt[q][:, k, :],
                                          start=(k == 0), stop=(k == KT - 1))
                        t.then_inc(score_mm, 1)
                        project(pe, n, xt[q], w0_sb, None, None, 0)

                    def body(i):
                        for q in (0, 1):
                            j = 2 * i + q
                            pe.wait_ge(x_in[q], 16 * (i + 1))
                            turn_tile(pe, j, xin[q])
                            if not (isinstance(i, int) and j == 0):
                                scores(j - 1, 1 - q)
                    pair_loop(pe, body, first=True)
                    scores(T - 1, 1)

                @block.scalar
                def _(act):
                    def scores_out(n, q, wait_row):
                        act.wait_ge(score_mm, n + 1)
                        act.activation(neg_t[0:P, n, :], sc[0:P, 0:H0], ACT.Copy, scale=-1.0).then_inc(score_out, 1)
                        wait(act, row_stored[q], wait_row)
                        act.activation(srow[q][:, :], sc[0:H0, 16:16 + P], ACT.Copy).then_inc(score_out, 1)

                    def body(i):
                        for q in (0, 1):
                            j = 2 * i + q
                            keep_turned(act, j, xt[q])
                            if not (isinstance(i, int) and j == 0):
                                scores_out(j - 1, 1 - q, 16 * (i if q else i - 1))
                    pair_loop(act, body, first=2)
                    scores_out(T - 1, 1, 16 * (PAIRS - 1))

                @block.vector
                def _(dve):
                    dve.memset(half[:, :], -0.5).then_inc(set_const, 1)
                    dve.memset(ones[:, :], 1.0).then_inc(set_const, 1)
                    dve.memset(u3s[:, :, :], 0.0).then_inc(set_const, 1)
                    dve.memset(u3n[:, :, :], 0.0).then_inc(set_const, 1)
                    for h in range(H0):
                        dve.memset(HA[:, :, h * FW + F0], 1.0).then_inc(set_const, 1)
                    done = [0, 0]

                    def fold(weights, vector, parts, width, dst, stock):
                        wait(dve, fold_sum, done[1])
                        for k in range(stock):
                            dve.tensor_tensor(tmp[:, k, :], weights(k), vector, ALU.mult).then_inc(fold_mul, 1)
                            done[0] += 1
                        dve.wait_ge(fold_mul, done[0])
                        dve.tensor_reduce(dst, tmp[:, 0:stock, :].rearrange("p k (h f) -> p (k h) f", f=width),
                                          AX.X, ALU.add).then_inc(fold_sum, 1)
                        done[1] += 1

                    dve.wait_ge(w_in, 16)
                    dve.wait_ge(vec_in, 48)
                    fold(lambda k: w0_sb[:, k, :], vecs[1], H0, F0, u0n[:, :, :].rearrange("p k h -> p (k h)"), KT)
                    fold(lambda k: w0_sb[:, k, :], vecs[0], H0, F0, u0s[:, :, :].rearrange("p k h -> p (k h)"), KT)
                    dve.wait_ge(u_in, 7 * 16)
                    dve.wait_ge(set_const, 4)
                    fold(lambda k: wld[:, k, :], vecs[2], 1, D, u2s[:, :, 0], KT)
                    fold(lambda k: wld[:, 4 + k, :], vecs[2], 1, D, u2n[:, :, 0], KT)
                    fold(lambda k: wld[:, 8, :], vecs[3], H3, D3,
                         u3s[:, :, :].rearrange("p k h -> p (k h)")[:, 0:KT * H3:H3 + 1], 1)
                    fold(lambda k: wld[:, 8, :], vecs[4], H3, D3,
                         u3n[:, :, :].rearrange("p k h -> p (k h)")[:, 0:KT * H3:H3 + 1], 1)
                    dve.wait_ge(set_const, 4 + H0)

                    def feats_out(n):
                        dve.wait_ge(proj_mm, n + 1)
                        dve.tensor_copy(HA[0:P, n, :].rearrange("p (h w) -> p h w", w=FW)[:, :, 0:F0],
                                        pj[0:P, :].rearrange("p (h f) -> p h f", f=F0)).then_inc(proj_out, 1)

                    def body(i):
                        for q in (0, 1):
                            j = 2 * i + q
                            dve.wait_ge(adj_in[q], 16 * (i + 1))
                            dve.tensor_scalar(msk[:, j, :], al[q][:, :], 0.0, FAR, ALU.is_le, ALU.mult)\
                               .then_inc(mask_done, 1)
                            if not (isinstance(i, int) and j == 0):
                                feats_out(j - 1)
                    pair_loop(dve, body, first=True)
                    feats_out(T - 1)

        with ExitStack() as ph:
            sB = [sb(ph, f"sB{q}", [P, CW]) for q in (0, 1)]
            dist = [sb(ph, f"dist{k}", [P, CW]) for k in range(4)]
            hf = [sb(ph, f"hf{q}", [P, T, FW]) for q in (0, 1)]
            hf_ready = sem("hf_ready")
            sums = sb(ph, "sums", [FW, CW])
            den = sb(ph, "den", [P, CT])
            rden = sb(ph, "rden", [P, CT])
            s_in = sems("s_in")
            d_ready, sq_act, sq_dve, p_ready, pv_done = (sem(k) for k in ("d_ready", "sq_act", "sq_dve", "p_ready", "pv_done"))
            sums_out, sums_turned = sem("sums_out"), sem("sums_turned")
            den_ready, rden_ready, head_out = sem("den_ready"), sem("rden_ready"), sem("head_out")
            n_act = sum(SQ_ON_ACT)
            n_dve = T - n_act

            EVAC_AT, TURN_AT, RESULT_AT = (3, 4, 5), 6, 12
            PARTS = [(a, min(a + 4, CT)) for a in range(0, CT, 4)]

            def sums_bank(hh, k):
                return bank[3 * hh + k]

            def group(c, hp, hh):
                return c * H0 + hp * 2 + hh

            def head_loop(eng, body, c, first):
                if first:
                    body(0)
                with eng.Fori(int(first), H0 // 2) as hp:
                    body(hp)

            with nc.Block() as block:
                @block.sync
                def _(sp):
                    for c in range(CH):
                        def body(hp):
                            for hh in (0, 1):
                                wait(sp, d_ready, (group(c, hp, hh) - 1) * T)
                                sp.dma_start(sB[hh][:, :],
                                             rows0[hp * 2 + hh, c * CW:(c + 1) * CW].partition_broadcast(P))\
                                  .then_inc(s_in[hh], 16)
                        head_loop(sp, body, c, True)

                @block.vector
                def _(dve):
                    def head_result(c, h, g):
                        a, b = bank[6], bank[7]
                        va = a[0:P, 0:TA * FW].rearrange("p (t w) -> p t w", w=FW)
                        vb = b[0:P, 0:(CT - TA) * FW].rearrange("p (t w) -> p t w", w=FW)
                        dve.wait_ge(sums_turned, g + 1)
                        dve.tensor_scalar(den[:, 0:TA], va[:, :, F0], EPS0, None, ALU.add).then_inc(den_ready, 1)
                        dve.tensor_scalar(den[:, TA:CT], vb[:, :, F0], EPS0, None, ALU.add).then_inc(den_ready, 1)
                        dve.wait_ge(den_ready, 2 * (g + 1))
                        dve.reciprocal(rden[:, :], den[:, :]).then_inc(rden_ready, 1)
                        dve.wait_ge(rden_ready, g + 1)
                        for v, lo, hi in ((va, 0, TA), (vb, TA, CT)):
                            dve.tensor_tensor(HB[0:P, c * CT + lo:c * CT + hi, bass.ds(h * F0, F0)], v[:, :, 0:F0],
                                              rden[:, lo:hi].unsqueeze(2).broadcast_to([P, hi - lo, F0]),
                                              ALU.mult).then_inc(head_out, 1)

                    for c in range(CH):
                        def body(hp):
                            for hh in (0, 1):
                                g = group(c, hp, hh)
                                dve.wait_ge(s_in[hh], 16 * (c * (H0 // 2) + hp + 1))
                                late = None
                                for m in range(T):
                                    s = g * T + m
                                    d = dist[(hh * T + m) % 4]
                                    wait(dve, pv_done, s - 3)
                                    if SQ_ON_ACT[m]:
                                        dve.tensor_tensor(d[:, :], msk[:, m, c * CW:(c + 1) * CW], sB[hh][:, :],
                                                          ALU.add).then_inc(d_ready, 1)
                                    else:
                                        dve.scalar_tensor_tensor(
                                            out=d[:, :], in0=msk[:, m, c * CW:(c + 1) * CW],
                                            scalar=neg_t[0:P, m, bass.ds(hp * 2 + hh, 1)], in1=sB[hh][:, :],
                                            op0=ALU.add, op1=ALU.add).then_inc(d_ready, 1)
                                    if late is not None:
                                        dve.wait_ge(d_ready, late[1] + 1)
                                        dve.tensor_tensor(late[0][:, :], late[0][:, :], late[0][:, :], ALU.mult)\
                                           .then_inc(sq_dve, 1)
                                        late = None
                                    if not SQ_ON_ACT[m]:
                                        late = (d, s)
                                    if m == RESULT_AT and not (isinstance(hp, int) and hp == 0 and c == 0 and hh == 0):
                                        if hh == 1:
                                            head_result(c, hp * 2, g - 1)
                                        elif isinstance(hp, int) and hp == 0:
                                            head_result(c - 1, H0 - 1, g - 1)
                                        else:
                                            head_result(c, hp * 2 - 1, g - 1)
                                if late is not None:
                                    dve.wait_ge(d_ready, late[1] + 1)
                                    dve.tensor_tensor(late[0][:, :], late[0][:, :], late[0][:, :], ALU.mult)\
                                       .then_inc(sq_dve, 1)
                        head_loop(dve, body, c, True)
                    head_result(CH - 1, H0 - 1, CH * H0 - 1)

                @block.gpsimd
                def _(pool):
                    for c in range(CH):
                        def body(hp):
                            for hh in (0, 1):
                                g = group(c, hp, hh)
                                wait(pool, pv_done, (g - 1) * T)
                                pool.tensor_copy(hf[hh][:, :, :], HA[0:P, :, bass.ds((hp * 2 + hh) * FW, FW)])\
                                    .then_inc(hf_ready, 1)
                        head_loop(pool, body, c, True)

                @block.scalar
                def _(act):
                    def evacuate(g, hh, k):
                        a, b = PARTS[k]
                        if k == 0:
                            act.wait_ge(pv_done, (g + 1) * T)
                            wait(act, sums_turned, g)
                        act.activation(sums[:, a * P:b * P], sums_bank(hh, k)[0:FW, 0:(b - a) * P], ACT.Copy)\
                           .then_inc(sums_out, 1)

                    for c in range(CH):
                        def body(hp):
                            for hh in (0, 1):
                                g = group(c, hp, hh)
                                first = isinstance(g, int) and g == 0

                                def square(m):
                                    if SQ_ON_ACT[m]:
                                        d = dist[(hh * T + m) % 4]
                                        act.wait_ge(d_ready, g * T + m + 1)
                                        act.activation(d[:, :], d[:, :], ACT.Square,
                                                       bias=neg_t[0:P, m, bass.ds(hp * 2 + hh, 1)]).then_inc(sq_act, 1)

                                def expo(m):
                                    d = dist[(hh * T + m) % 4]
                                    if SQ_ON_ACT[m]:
                                        act.wait_ge(sq_act, g * n_act + sum(SQ_ON_ACT[:m + 1]))
                                    else:
                                        act.wait_ge(sq_dve, g * n_dve + (m + 1 - sum(SQ_ON_ACT[:m + 1])))
                                    act.activation(d[:, :], d[:, :], ACT.Exp, scale=-1.0).then_inc(p_ready, 1)

                                square(0)
                                for m in range(T):
                                    if m + 1 < T:
                                        square(m + 1)
                                    expo(m)
                                    if m in EVAC_AT and not first:
                                        evacuate(g - 1, 1 - hh, EVAC_AT.index(m))
                        head_loop(act, body, c, c == 0)
                    for k in range(len(PARTS)):
                        evacuate(CH * H0 - 1, 1, k)

                @block.tensor
                def _(pe):
                    def turn_sums(g):
                        pe.wait_ge(sums_out, len(PARTS) * (g + 1))
                        wait(pe, head_out, 2 * g)
                        for t in range(CT):
                            o = (t - TA if t >= TA else t) * FW
                            mm = pe.transpose(bank[6 + (t >= TA)][0:P, o:o + FW], sums[:, t * P:(t + 1) * P],
                                              idt[0:FW, 0:FW])
                        mm.then_inc(sums_turned, 1)

                    for c in range(CH):
                        def body(hp):
                            for hh in (0, 1):
                                g = group(c, hp, hh)
                                for m in range(T):
                                    if m == 0:
                                        pe.wait_ge(hf_ready, g + 1)
                                        wait(pe, sums_out, len(PARTS) * (g - 1))
                                    pe.wait_ge(p_ready, g * T + m + 1)
                                    d = dist[(hh * T + m) % 4]
                                    for k, (a, b) in enumerate(PARTS):
                                        mm = pe.matmul(sums_bank(hh, k)[0:FW, 0:(b - a) * P], hf[hh][:, m, :],
                                                       d[:, a * P:b * P], start=(m == 0), stop=(m == T - 1))
                                    mm.then_inc(pv_done, 1)
                                    if m == TURN_AT and not (isinstance(g, int) and g == 0):
                                        turn_sums(g - 1)
                        head_loop(pe, body, c, True)
                    turn_sums(CH * H0 - 1)
        msk_stack.close()

        def norm_buffers(ph):
            R = [sb(ph, f"R{q}", [P, D]) for q in (0, 1)]
            xn = [sb(ph, f"xn{q}", [P, D]) for q in (0, 1)]
            st = [sb(ph, f"st{q}", [P, 10]) for q in (0, 1)]
            xin = [sb(ph, f"xin{q}", [P, D]) for q in (0, 1)]
            xt = [sb(ph, f"xt{q}", [128, KT, P]) for q in (0, 1)]
            bias = sb(ph, "bias", [P, D])
            w_sb = sb(ph, "w_sb", [128, KT, D])
            return R, xn, st, xin, xt, bias, w_sb

        def norm_store(pool, i, q, n, dst, st, xn):
            ln_power(pool, n, q, st)
            pool.wait_ge(ln_done, n + 1)
            pool.dma_start(dst[2 * i + q], xn[q][:, :]).then_inc(xn_stored[q], 16)

        def normed(dve, n, i, q, R, st, xn, phase):
            ln_tile(dve, n, q, R, st, xn)
            wait(dve, xn_stored[q], 16 * (phase * PAIRS + i))
            wait(dve, turned, n + T - 1)
            ln_write(dve, n, q, R, st, xn[q][:, :])

        with ExitStack() as ph:
            R, xn, st, xin, xt, bias, w_sb = norm_buffers(ph)
            c_in = sem("e0_in")
            with nc.Block() as block:
                @block.sync
                def _(sp):
                    sp.dma_start(bias[:, :], b0.partition_broadcast(P)).then_inc(c_in, 16)
                    sp.dma_start(w_sb[:, :, :], w1).then_inc(c_in, 16)

                    def body(i):
                        for q in (0, 1):
                            wait(sp, r_full, 2 * i + q - 1)
                            sp.dma_start(xin[q][:, :], x[2 * i + q]).then_inc(x_in[q], 16)
                    pair_loop(sp, body, first=True)

                @block.vector
                def _(dve):
                    dve.wait_ge(c_in, 32)

                    def body(i):
                        for q in (0, 1):
                            j = 2 * i + q
                            dve.tensor_tensor(R[q][:, :], HB[0:P, j, :], bias[:, :], ALU.add).then_inc(r_half, 1)
                            dve.wait_ge(r_half, j + 1)
                            dve.wait_ge(x_in[q], 16 * (PAIRS + i + 1))
                            dve.scalar_tensor_tensor(out=R[q][:, :], in0=R[q][:, :], scalar=0.0, in1=xin[q][:, :],
                                                     op0=ALU.max, op1=ALU.add).then_inc(r_full, 1)
                            normed(dve, j, i, q, R, st, xn, 0)
                            if not (isinstance(i, int) and j == 0):
                                h_out(j - 1)

                    def h_out(j):
                        dve.wait_ge(proj_mm, T + j + 1)
                        dve.tensor_copy(HA[0:P, j, 0:D], pj[0:P, :]).then_inc(proj_out, 1)
                    pair_loop(dve, body, first=True)
                    h_out(T - 1)

                @block.gpsimd
                def _(pool):
                    def body(i):
                        for q in (0, 1):
                            norm_store(pool, i, q, 2 * i + q, xs[0], st, xn)
                    pair_loop(pool, body)
                    for q in (0, 1):
                        pool.wait_ge(xn_stored[q], 16 * PAIRS)

                @block.tensor
                def _(pe):
                    pe.wait_ge(c_in, 32)

                    def body(i):
                        for q in (0, 1):
                            j = 2 * i + q
                            pe.wait_ge(ln_done, j + 1)
                            turn_tile(pe, T + j, xn[q])
                            project(pe, T + j, xt[q], w_sb, None, None, 0)
                    pair_loop(pe, body)

                @block.scalar
                def _(act):
                    def body(i):
                        for q in (0, 1):
                            keep_turned(act, T + 2 * i + q, xt[q])
                    pair_loop(act, body)

        with ExitStack() as ph:
            R, xn, st, xin, xt, bias, w_sb = norm_buffers(ph)
            at = [sb(ph, f"at{q}", [P, T, P]) for q in (0, 1)]
            vb = sb(ph, "vb", [P, D])
            srow = [sb(ph, f"srow{q}", [1, P]) for q in (0, 1)]
            c_in, at_in, agg_done = sem("l1_in"), sems("at_in"), sem("agg_done")
            with nc.Block() as block:
                @block.sync
                def _(sp):
                    sp.dma_start(bias[:, :], b1.partition_broadcast(P)).then_inc(c_in, 16)
                    sp.dma_start(w_sb[:, :, :], fc_w).then_inc(c_in, 16)
                    sp.dma_start(vb[:, :], fc_b.partition_broadcast(P)).then_inc(c_in, 16)

                    def body(i):
                        for q in (0, 1):
                            j = 2 * i + q
                            wait(sp, agg_done, j - 1)
                            sp.dma_start(at[q][:, :, :], adj_tiles[j]).then_inc(at_in[q], 16)
                            wait(sp, r_full, T + j - 1)
                            sp.dma_start(xin[q][:, :], xs[0][j]).then_inc(x_in[q], 16)
                    pair_loop(sp, body, first=True)

                @block.tensor
                def _(pe):
                    pe.wait_ge(c_in, 48)

                    def tail(j, q, part):
                        n = 2 * T + j
                        if part == 0:
                            pe.wait_ge(ln_done, T + j + 1)
                            turn_tile(pe, n, xn[q])
                        else:
                            scores(n, j, q)

                    def scores(n, j, q):
                        pe.wait_ge(turned_out, n + 1)
                        wait(pe, score_out, 2 * (T + j))
                        for k in range(KT):
                            pe.matmul(sc[0:P, 0:1], xt[q][:, k, :], u2s[:, k, :], start=(k == 0), stop=(k == KT - 1))
                        for k in range(KT):
                            t = pe.matmul(sc[0:1, 16:16 + P], u2n[:, k, :], xt[q][:, k, :],
                                          start=(k == 0), stop=(k == KT - 1))
                        t.then_inc(score_mm, 1)
                        project(pe, n, xt[q], w_sb, None, None, 0)

                    def body(i):
                        for q in (0, 1):
                            j = 2 * i + q
                            pe.wait_ge(at_in[q], 16 * (i + 1))
                            wait(pe, r_half, T + j - 1)
                            for m in range(T):
                                mm = pe.matmul(acc[q][0:P, :], at[q][:, m, :], HA[0:P, m, 0:D],
                                               start=(m == 0), stop=(m == T - 1))
                                if not (isinstance(i, int) and j == 0) and m in (9, 17):
                                    tail(j - 1, 1 - q, int(m == 17))
                            mm.then_inc(agg_done, 1)
                    pair_loop(pe, body, first=True)
                    tail(T - 1, 1, 0)
                    tail(T - 1, 1, 1)

                @block.vector
                def _(dve):
                    dve.wait_ge(c_in, 48)

                    def v_out(j):
                        dve.wait_ge(proj_mm, 2 * T + j + 1)
                        dve.tensor_tensor(HB[0:P, j, :], pj[0:P, :], vb[:, :], ALU.add).then_inc(proj_out, 1)

                    def body(i):
                        for q in (0, 1):
                            j = 2 * i + q
                            n = T + j
                            dve.wait_ge(agg_done, j + 1)
                            dve.tensor_tensor(R[q][:, :], acc[q][0:P, :], bias[:, :], ALU.add).then_inc(r_half, 1)
                            dve.wait_ge(r_half, n + 1)
                            dve.wait_ge(x_in[q], 16 * (2 * PAIRS + i + 1))
                            dve.tensor_tensor(R[q][:, :], R[q][:, :], xin[q][:, :], ALU.add).then_inc(r_full, 1)
                            ln_tile(dve, n, q, R, st, xn)
                            wait(dve, xn_stored[q], 16 * (PAIRS + i))
                            wait(dve, turned, n + T - 1)
                            ln_write(dve, n, q, R, st, xn[q][:, :])
                            v_out(j)
                    pair_loop(dve, body)

                @block.gpsimd
                def _(pool):
                    def body(i):
                        for q in (0, 1):
                            j = 2 * i + q
                            norm_store(pool, i, q, T + j, xs[1], st, xn)
                            pool.wait_ge(score_out, 2 * (T + j) + 2)
                            pool.dma_start(rows2[:, bass.ds(j * P, P)], srow[q][:, :]).then_inc(row_stored[q], 16)
                    pair_loop(pool, body)
                    for q in (0, 1):
                        pool.wait_ge(xn_stored[q], 16 * 2 * PAIRS)
                        pool.wait_ge(row_stored[q], 16 * 2 * PAIRS)

                @block.scalar
                def _(act):
                    def body(i):
                        for q in (0, 1):
                            j = 2 * i + q
                            keep_turned(act, 2 * T + j, xt[q])
                            act.wait_ge(score_mm, T + j + 1)
                            act.activation(s1[0:P, bass.ds(j, 1)], sc[0:P, 0:1], ACT.Identity, bias=ab2[0:P, :])\
                               .then_inc(score_out, 1)
                            act.wait_ge(row_stored[q], 16 * (PAIRS + i))
                            act.activation(srow[q][:, :], sc[0:1, 16:16 + P], ACT.Copy).then_inc(score_out, 1)
                    pair_loop(act, body)

        with ExitStack() as ph:
            R, xn, st, xin, xt, _, w_sb = norm_buffers(ph)
            rows = [sb(ph, f"rows{q}", [P, NP]) for q in (0, 1)]
            pr = [sb(ph, f"pr{q}", [P, NP]) for q in (0, 1)]
            pt = [sb(ph, f"pt{q}", [P, T, P]) for q in (0, 1)]
            sB2 = sb(ph, "sB2", [P, NP])
            stat = [sb(ph, f"stat{q}", [P, 4]) for q in (0, 1)]
            sums = sb(ph, "sums", [P, T])
            srow = [sb(ph, f"srow{q}", [H3, P]) for q in (0, 1)]
            c_in, rows_in = sem("l2_in"), sems("l2_rows_in")
            neg_ready, z_ready, leaky_ready, max_ready, nmax_ready, p2_ready, rsum_ready = (
                sem(f"l2_{k}") for k in ("neg", "z", "leaky", "max", "nmax", "p", "rsum"))
            t_grp, t_out, m_grp = sem("l2_t_grp"), sem("l2_t_out"), sem("l2_m_grp")
            with nc.Block() as block:
                @block.sync
                def _(sp):
                    sp.dma_start(sB2[:, :], rows2[0, :].partition_broadcast(P)).then_inc(c_in, 16)
                    sp.dma_start(w_sb[:, 0, :], w3).then_inc(c_in, 16)

                    def body(i):
                        for q in (0, 1):
                            j = 2 * i + q
                            wait(sp, max_ready, j - 1)
                            sp.dma_start(rows[q][:, :], adj_rows[j]).then_inc(rows_in[q], 16)
                            wait(sp, r_full, 2 * T + j - 1)
                            sp.dma_start(xin[q][:, :], xs[1][j]).then_inc(x_in[q], 16)
                    pair_loop(sp, body, first=True)

                @block.scalar
                def _(act):
                    act.wait_ge(c_in, 32)

                    def z(j, q):
                        wait(act, t_grp, NG * (j - 1))
                        act.activation(pr[q][:, :], sB2[:, :], ACT.Identity, bias=s1[0:P, bass.ds(j, 1)])\
                           .then_inc(z_ready, 1)

                    def expo(j, q):
                        act.wait_ge(nmax_ready, j + 1)
                        act.activation(pr[q][:, :], pr[q][:, :], ACT.Exp, bias=stat[q][:, 1:2],
                                       accum_out=sums[:, bass.ds(j, 1)]).then_inc(p2_ready, 1)

                    def tail(j, q):
                        keep_turned(act, 3 * T + j, xt[q])
                        act.wait_ge(score_mm, 2 * T + j + 1)
                        act.activation(f1[0:P, j, :], sc[0:P, 0:H3], ACT.Copy).then_inc(score_out, 1)
                        act.wait_ge(row_stored[q], 16 * (2 * PAIRS + (j - q) // 2) if isinstance(j, int)
                                    else 16 * (2 * PAIRS) + (j - q) * 8)
                        act.activation(srow[q][:, :], sc[0:H3, 16:16 + P], ACT.Copy).then_inc(score_out, 1)

                    def body(i):
                        for q in (0, 1):
                            j = 2 * i + q
                            if not (isinstance(i, int) and j + 2 >= T):
                                z(j + 2, q)
                                expo(j + 2, q)
                            if not (isinstance(i, int) and j == 0):
                                tail(j - 1, 1 - q)
                    for j in (0, 1):
                        z(j, j)
                        expo(j, j)
                    pair_loop(act, body, first=True, last=True)
                    tail(T - 1, 1)

                @block.vector
                def _(dve):
                    def missing(j, i, q):
                        dve.wait_ge(rows_in[q], 16 * (i + 1))
                        dve.tensor_scalar(rows[q][:, 0:N], rows[q][:, 0:N], 0.0, NEG, ALU.is_le, ALU.mult)\
                           .then_inc(neg_ready, 1)
                        dve.memset(rows[q][:, N:NP], LOW).then_inc(neg_ready, 1)

                    def leaky(j, q):
                        dve.wait_ge(z_ready, j + 1)
                        dve.scalar_tensor_tensor(out=pr[q][:, :], in0=pr[q][:, :], scalar=0.2, in1=pr[q][:, :],
                                                 op0=ALU.mult, op1=ALU.max).then_inc(leaky_ready, 1)

                    def masked_max(j, q):
                        scored, masked = count(dve, j + 1), count(dve, 2 * j + 2)
                        carry(dve, set_const, 1)
                        dve.wait_ge(leaky_ready, scored)
                        dve.wait_ge(neg_ready, masked)
                        dve.tensor_tensor_reduce(pr[q][:, :], pr[q][:, :], rows[q][:, :], 1.0, LOW, ALU.add, ALU.max,
                                                 stat[q][:, 0:1]).then_inc(max_ready, 1)
                        dve.wait_ge(max_ready, j + 1)
                        dve.tensor_scalar(stat[q][:, 1:2], stat[q][:, 0:1], -1.0, None, ALU.mult)\
                           .then_inc(nmax_ready, 1)

                    def keep(j, g):
                        u = NG * j + g
                        a, b = GROUPS[g]
                        dve.wait_ge(t_grp, u + 1)
                        wait(dve, m_grp, u - 2 * NG + 1)
                        dve.tensor_copy(pt[par(j)][:, a:b, :],
                                        turn[g % 3][0:P, 0:(b - a) * P].rearrange("p (t n) -> p t n", n=P))\
                           .then_inc(t_out, 1)

                    parity = {}

                    def par(j):
                        return j % 2 if isinstance(j, int) else parity["q"]

                    def result(j, q):
                        n = 2 * T + j
                        dve.wait_ge(m_grp, NG * (j + 1))
                        dve.wait_ge(p2_ready, j + 1)
                        dve.reciprocal(stat[q][:, 3:4], sums[:, bass.ds(j, 1)]).then_inc(rsum_ready, 1)
                        dve.wait_ge(rsum_ready, j + 1)
                        dve.wait_ge(x_in[q], (16 * 3 * PAIRS + 16 * (j - q) // 2 + 16) if isinstance(j, int)
                                    else (j - q) * 8 + 16 * 3 * PAIRS + 16)
                        dve.scalar_tensor_tensor(out=R[q][:, :], in0=acc[q][0:P, :], scalar=stat[q][:, 3:4],
                                                 in1=xin[q][:, :], op0=ALU.mult, op1=ALU.add).then_inc(r_full, 1)
                        ln_tile(dve, n, q, R, st, xn)
                        wait(dve, xn_stored[q], (16 * 2 * PAIRS + 8 * (j - q)) if isinstance(j, int)
                             else (j - q) * 8 + 16 * 2 * PAIRS)
                        wait(dve, turned, n + T - 1)
                        ln_write(dve, n, q, R, st, xn[q][:, :])

                    def v_out(j):
                        dve.wait_ge(proj_mm, 3 * T + j + 1)
                        dve.tensor_copy(HA[0:P, j, 0:D], pj[0:P, :]).then_inc(proj_out, 1)

                    for j in (0, 1):
                        missing(j, 0, j)
                        leaky(j, j)
                        masked_max(j, j)
                    for g in range(NG):
                        keep(0, g)

                    def body(i):
                        for q in (0, 1):
                            j = 2 * i + q
                            head = isinstance(i, int) and j == 0
                            ahead = not (isinstance(i, int) and j + 2 >= T)
                            for g in range(NG):
                                if not (isinstance(i, int) and j + 1 >= T):
                                    parity["q"] = 1 - q
                                    keep(j + 1, g)
                                if g == 0 and not head:
                                    result(j - 1, 1 - q)
                                if g == 1 and ahead:
                                    missing(j + 2, i + 1, q)
                                if g == 2 and ahead:
                                    leaky(j + 2, q)
                                if g == 4 and ahead:
                                    masked_max(j + 2, q)
                                if g == 5 and not head:
                                    v_out(j - 1)
                    pair_loop(dve, body, first=True, last=True)
                    result(T - 1, 1)
                    v_out(T - 1)

                @block.tensor
                def _(pe):
                    pe.wait_ge(c_in, 32)

                    def turn_group(j, q, g):
                        u = NG * j + g
                        a, b = GROUPS[g]
                        if g == 0:
                            pe.wait_ge(p2_ready, j + 1)
                        wait(pe, t_out, u - 2)
                        for m in range(a, b):
                            t = pe.transpose(turn[g % 3][0:P, (m - a) * P:(m - a + 1) * P],
                                             pr[q][:, m * P:(m + 1) * P], idt[0:P, 0:P])
                        t.then_inc(t_grp, 1)

                    def mul_group(j, q, g):
                        a, b = GROUPS[g]
                        pe.wait_ge(t_out, NG * j + g + 1)
                        if g == 0:
                            wait(pe, r_full, 2 * T + j - 1)
                        for m in range(a, b):
                            t = pe.matmul(acc[q][0:P, :], pt[q][:, m, :], HB[0:P, m, :],
                                          start=(m == 0), stop=(m == T - 1))
                        t.then_inc(m_grp, 1)

                    def tail(j, q, part):
                        n = 3 * T + j
                        if part == 0:
                            pe.wait_ge(ln_done, 2 * T + j + 1)
                            turn_tile(pe, n, xn[q])
                            return
                        pe.wait_ge(turned_out, n + 1)
                        wait(pe, score_out, 2 * (2 * T + j))
                        for k in range(KT):
                            pe.matmul(sc[0:P, 0:H3], xt[q][:, k, :], u3s[:, k, :], start=(k == 0), stop=(k == KT - 1))
                        for k in range(KT):
                            t = pe.matmul(sc[0:H3, 16:16 + P], u3n[:, k, :], xt[q][:, k, :],
                                          start=(k == 0), stop=(k == KT - 1))
                        t.then_inc(score_mm, 1)
                        project(pe, n, xt[q], w_sb[:, 0, :].rearrange("p (h e) -> p h e", e=D3), None, None, 0,
                                blocked=True)

                    for g in range(NG):
                        turn_group(0, 0, g)

                    def body(i):
                        for q in (0, 1):
                            j = 2 * i + q
                            head = isinstance(i, int) and j == 0
                            for g in range(NG):
                                if not (isinstance(i, int) and j + 1 >= T):
                                    turn_group(j + 1, 1 - q, g)
                                mul_group(j, q, g)
                                if g == 2 and not head:
                                    tail(j - 1, 1 - q, 0)
                                if g == 4 and not head:
                                    tail(j - 1, 1 - q, 1)
                    pair_loop(pe, body, first=True, last=True)
                    tail(T - 1, 1, 0)
                    tail(T - 1, 1, 1)

                @block.gpsimd
                def _(pool):
                    def body(i):
                        for q in (0, 1):
                            j = 2 * i + q
                            norm_store(pool, i, q, 2 * T + j, xs[2], st, xn)
                            pool.wait_ge(score_out, 2 * (2 * T + j) + 2)
                            pool.dma_start(rows3[:, bass.ds(j * P, P)], srow[q][:, :]).then_inc(row_stored[q], 16)
                    pair_loop(pool, body)
                    for q in (0, 1):
                        pool.wait_ge(xn_stored[q], 16 * 3 * PAIRS)
                        pool.wait_ge(row_stored[q], 16 * 3 * PAIRS)
        L0.close()

        a_bn = [sb(top, f"a_bn{k}", [P, D]) for k in range(2)]
        shift = sb(top, "shift", [P, D])
        lin, quad = sb(top, "lin", [P, D]), sb(top, "quad", [P, D])
        shift_mm, shift_ready = sem("shift_mm"), sem("shift_ready")
        st_y, st_lin, st_sq, st_quad = (sem(f"stats_{k}") for k in ("y", "lin", "sq", "quad"))
        bn_zero, bn_sum, bn_step, bn_pow, bn_row = (sem(f"bn_{k}") for k in ("zero", "sum", "step", "pow", "row"))
        xc_ready, row_out, gb_in = sem("xc_ready"), sem("bn_row_out"), sem("gb_in")
        gb = sb(top, "gb", [128, 2, 3, KT])
        bnf = sb(top, "bnf", [128, 4, KT])

        def stats_tile(pool, n, y, src, count):
            pool.wait_ge(xc_ready, n + 1)
            pool.tensor_tensor(y[0][0:count, :], src, shift[0:count, :], ALU.subtract).then_inc(st_y, 1)
            pool.wait_ge(st_y, n + 1)
            wait(pool, st_lin, n)
            pool.tensor_tensor(lin[0:count, :], lin[0:count, :], y[0][0:count, :], ALU.add).then_inc(st_lin, 1)
            pool.tensor_tensor(y[1][0:count, :], y[0][0:count, :], y[0][0:count, :], ALU.mult).then_inc(st_sq, 1)
            pool.wait_ge(st_sq, n + 1)
            wait(pool, st_quad, n)
            pool.tensor_tensor(quad[0:count, :], quad[0:count, :], y[1][0:count, :], ALU.add).then_inc(st_quad, 1)

        def shift_matmul(pe, k, src):
            pe.wait_ge(xc_ready, k * T + 1)
            pe.matmul(bank[7][0:P, :], ones[0:P, 0:P], src, start=True, stop=True).then_inc(shift_mm, 1)

        def shift_out(dve, k):
            dve.wait_ge(shift_mm, k + 1)
            dve.tensor_scalar(shift[:, :], bank[7][0:P, :], 1.0 / P, None, ALU.mult).then_inc(shift_ready, 1)

        def sums_clear(pool, k):
            pool.memset(lin[:, :], 0.0).then_inc(bn_zero, 1)
            pool.memset(quad[:, :], 0.0).then_inc(bn_zero, 1)
            pool.wait_ge(bn_zero, 2 * k + 2)

        def bn_total(pe, k):
            pe.wait_ge(st_quad, (k + 1) * T)
            pe.wait_ge(st_lin, (k + 1) * T)
            for part, src in enumerate((lin, quad, shift)):
                for c in range(KT):
                    t = pe.matmul(bank[6][:, part * KT + c:part * KT + c + 1], src[:, c * 128:(c + 1) * 128],
                                  ones[0:P, 0:1], start=True, stop=True)
            t.then_inc(bn_sum, 1)
            for part in range(2):
                pe.wait_ge(bn_step, 8 * k + 6 + 2 * part)
                for c in range(KT):
                    t = pe.matmul(bank[7 - part][0:P, c * 128:(c + 1) * 128],
                                  bnf[:, part, c:c + 1].broadcast_to([128, P]), idt[:, :], start=True, stop=True)
                t.then_inc(bn_row, 1)

        def bn_finish(dve, k):
            f = [8 * k]
            scale, offset, mean, var = (bnf[:, c, :] for c in range(4))
            total = [bank[6][:, c * KT:(c + 1) * KT] for c in range(3)]

            def step(ins):
                ins.then_inc(bn_step, 1)
                f[0] += 1
                dve.wait_ge(bn_step, f[0])
            dve.wait_ge(bn_sum, k + 1)
            step(dve.tensor_scalar(mean, total[0], 1.0 / N, None, ALU.mult))
            step(dve.tensor_tensor(var, mean, mean, ALU.mult))
            step(dve.scalar_tensor_tensor(out=var, in0=total[1], scalar=1.0 / N, in1=var,
                                          op0=ALU.mult, op1=ALU.subtract))
            step(dve.tensor_scalar(var, var, BN_EPS, None, ALU.add))
            step(dve.scalar_tensor_tensor(out=mean, in0=total[2], scalar=1.0 / P, in1=mean,
                                          op0=ALU.mult, op1=ALU.add))
            dve.wait_ge(bn_pow, k + 1)
            dve.wait_ge(gb_in, 32)
            step(dve.tensor_tensor(scale, gb[:, 0, k, :], var, ALU.mult))
            step(dve.tensor_tensor(mean, mean, scale, ALU.mult))
            step(dve.tensor_tensor(offset, gb[:, 1, k, :], mean, ALU.subtract))
            for part in range(2):
                dve.wait_ge(bn_row, 2 * k + part + 1)
                dve.tensor_copy(a_bn[part][:, :], bank[7 - part][0:P, :]).then_inc(row_out, 1)
            dve.wait_ge(row_out, 2 * k + 2)

        def bn_power(pool, k):
            pool.wait_ge(bn_step, 8 * k + 4)
            pool.tensor_tensor(bnf[:, 3, :], bnf[:, 3, :], half[:, 0:1].broadcast_to([128, KT]), ALU.pow)\
                .then_inc(bn_pow, 1)

        weights = scratch("weights", [H3 * T, P, T, P])
        edge_ready = sem("edge_ready")
        ri = sb(top, "ri", [P, T, H3])
        has_edge = sb(top, "has_edge", [P, T])
        with ExitStack() as ph:
            rows = [sb(ph, f"rows{q}", [P, NP]) for q in (0, 1)]
            low = [sb(ph, f"low{q}", [P, NP // 4]) for q in (0, 1)]
            fB = sb(ph, "fB", [P, H3, NP])
            v = [sb(ph, f"v{h}", [P, NP]) for h in range(H3)]
            pt = [sb(ph, f"pt{q}", [P, T, P]) for q in (0, 1)]
            mx = [sb(ph, f"mx{q}", [P, H3]) for q in (0, 1)]
            nm, rs, rc = (sb(ph, n_, [P, T, H3]) for n_ in ("nm", "rs", "rc"))
            xc = [sb(ph, f"xc{q}", [P, D]) for q in (0, 1)]
            y = [sb(ph, f"y{k}", [P, D]) for k in (0, 1)]
            fb_in, rows_in = sem("att_in"), sems("att_rows_in")
            low_ready, adj_ready, sig_ready, mx_ready, nm_ready, p_ready = (
                sem(f"att_{k}") for k in ("low", "adj", "sig", "mx", "nm", "p"))
            t_grp, t_out, m_grp = sem("att_t_grp"), sem("att_t_out"), sem("att_m_grp")
            rc_ready, ri_ready, att_out = sem("att_rc"), sem("att_ri"), sem("att_att")
            stored = sems("att_stored")
            C4 = NP // 4
            weights_stored = sems("weights_stored")
            with nc.Block() as block:
                @block.sync
                def _(sp):
                    sp.dma_start(fB[:, :, :], rows3.partition_broadcast(P)).then_inc(fb_in, 16)
                    sp.dma_start(gb[:, 0, :, :], g_bn).then_inc(gb_in, 16)
                    sp.dma_start(gb[:, 1, :, :], b_bn).then_inc(gb_in, 16)

                    def load(i, q):
                        wait(sp, mx_ready, H3 * (2 * i + q - 1))
                        sp.dma_start(rows[q][:, :], adj_rows[2 * i + q]).then_inc(rows_in[q], 16)

                    def store(j, q):
                        sp.wait_ge(xc_ready, j + 1)
                        sp.dma_start(xc_dram[j], xc[q][:, :]).then_inc(stored[q], 16)

                    def body(i):
                        for q in (0, 1):
                            if not (isinstance(i, int) and i + 1 >= PAIRS):
                                load(i + 1, q)
                            if not (isinstance(i, int) and 2 * i + q == 0):
                                store(2 * i + q - 1, 1 - q)
                            for h in range(H3):
                                s = H3 * (2 * i + q) + h
                                sp.wait_ge(t_out, NG * (s + 1))
                                sp.dma_start(weights[s], pt[h % 2][:, :, :]).then_inc(weights_stored[h % 2], 16)
                    load(0, 0)
                    load(0, 1)
                    pair_loop(sp, body, first=True, last=True)
                    store(T - 1, 1)
                    for q in (0, 1):
                        sp.wait_ge(stored[q], 16 * PAIRS)
                        sp.wait_ge(weights_stored[q], 16 * H3 * PAIRS)

                @block.gpsimd
                def _(pool):
                    def absent(i, q):
                        j = 2 * i + q
                        loaded = count(pool, 16 * (i + 1))
                        carry(pool, set_const, 1)
                        pool.wait_ge(rows_in[q], loaded)
                        for c in range(4):
                            part = rows[q][:, c * C4:(c + 1) * C4]
                            pool.tensor_scalar(low[c % 2][:, :], part, 0.0, LOW, ALU.is_equal, ALU.mult)\
                                .then_inc(low_ready, 1)
                            pool.wait_ge(low_ready, 4 * j + c + 1)
                            pool.tensor_tensor(part, part, low[c % 2][:, :], ALU.add).then_inc(adj_ready, 1)

                    def tile_stats(j, q, count=P):
                        if isinstance(j, int) and j == 0:
                            pool.wait_ge(shift_ready, 1)
                        stats_tile(pool, j, y, xc[q][0:count, :], count)

                    def body(i):
                        for q in (0, 1):
                            j = 2 * i + q
                            if not (isinstance(i, int) and j == 0):
                                tile_stats(j - 1, 1 - q)
                            if not (isinstance(i, int) and i + 1 >= PAIRS):
                                absent(i + 1, q)
                    absent(0, 0)
                    absent(0, 1)
                    sums_clear(pool, 0)
                    pair_loop(pool, body, first=True, last=True)
                    tile_stats(T - 1, 1, TAIL)
                    bn_power(pool, 0)

                @block.scalar
                def _(act):
                    act.wait_ge(fb_in, 16)

                    def body(i):
                        for q in (0, 1):
                            j = 2 * i + q
                            for h in range(H3):
                                wait(act, t_grp, NG * (H3 * (j - 1) + h + 1))
                                act.activation(v[h][:, :], fB[:, h, :], ACT.Sigmoid, bias=f1[0:P, j, h:h + 1])\
                                   .then_inc(sig_ready, 1)
                            for h in range(H3):
                                act.wait_ge(nm_ready, H3 * j + h + 1)
                                act.activation(v[h][:, :], v[h][:, :], ACT.Exp, bias=nm[:, j, h:h + 1],
                                               accum_out=rs[:, j, h:h + 1]).then_inc(p_ready, 1)
                    pair_loop(act, body, first=True)

                @block.vector
                def _(dve):
                    def weigh(j, q, h):
                        s = H3 * j + h
                        masked, scored = count(dve, 4 * (j + 1)), count(dve, s + 1)
                        carry(dve, set_const, 1)
                        if h == 0:
                            dve.wait_ge(adj_ready, masked)
                        dve.wait_ge(sig_ready, scored)
                        dve.tensor_tensor_reduce(v[h][:, :], v[h][:, :], rows[q][:, :], 1.0, LOW, ALU.mult, ALU.max,
                                                 mx[q][:, h:h + 1]).then_inc(mx_ready, 1)
                        dve.wait_ge(mx_ready, s + 1)
                        dve.tensor_scalar(nm[:, j, h:h + 1], mx[q][:, h:h + 1], -1.0, None, ALU.mult)\
                           .then_inc(nm_ready, 1)

                    def keep(s, g, k):
                        u = NG * s + g
                        a, b = GROUPS[g]
                        dve.wait_ge(t_grp, u + 1)
                        wait(dve, m_grp, u - 2 * NG + 1)
                        if g == 0:
                            stores = s // 2 if isinstance(s, int) else 8 * s - 8 * k
                            wait(dve, weights_stored[k], 16 * stores if isinstance(s, int) else stores)
                        dve.tensor_copy(pt[k][:, a:b, :],
                                        turn[g % 3][0:P, 0:(b - a) * P].rearrange("p (t n) -> p t n", n=P))\
                           .then_inc(t_out, 1)

                    def result(j, q):
                        dve.wait_ge(p_ready, H3 * (j + 1))
                        dve.reciprocal(rc[:, j, :], rs[:, j, :]).then_inc(rc_ready, 1)
                        dve.wait_ge(rc_ready, j + 1)
                        dve.scalar_tensor_tensor(out=ri[:, j, :], in0=nm[:, j, :], scalar=1e20, in1=rc[:, j, :],
                                                 op0=ALU.is_lt, op1=ALU.mult).then_inc(ri_ready, 1)
                        dve.wait_ge(ri_ready, j + 1)
                        dve.wait_ge(m_grp, NG * H3 * (j + 1))
                        if isinstance(j, int):
                            wait(dve, stored[q], 16 * (j // 2))
                        else:
                            dve.wait_ge(stored[q], (j - q) * 8)
                        wait(dve, st_y, j - 1)
                        dve.tensor_tensor(xc[q][:, :].rearrange("p (h e) -> p h e", e=D3),
                                          acc[q][0:P, :].rearrange("p (h e) -> p h e", e=D3),
                                          ri[:, j, :].unsqueeze(2).broadcast_to([P, H3, D3]),
                                          ALU.mult).then_inc(xc_ready, 1)

                    for h in range(H3):
                        weigh(0, 0, h)
                    for g in range(NG):
                        keep(0, g, 0)

                    def body(i):
                        for q in (0, 1):
                            j = 2 * i + q
                            head = isinstance(i, int) and j == 0
                            final = isinstance(i, int) and j == T - 1
                            for h in range(H3):
                                if h == H3 - 1 and not final:
                                    weigh(j + 1, 1 - q, h)
                                for g in range(NG):
                                    if not (final and h == H3 - 1):
                                        keep(H3 * j + h + 1, g, (h + 1) % 2)
                                    if h == 0 and g == 1 and not head:
                                        result(j - 1, 1 - q)
                                    if isinstance(i, int) and j == 1 and h == 1 and g == 1:
                                        shift_out(dve, 0)
                                    if g == 2 and h < H3 - 1 and not final:
                                        weigh(j + 1, 1 - q, h)
                    pair_loop(dve, body, first=2, last=True)
                    result(T - 1, 1)
                    dve.tensor_scalar(has_edge[:, :], nm[:, :, 0], 1e20, None, ALU.is_lt).then_inc(edge_ready, 1)
                    dve.wait_ge(edge_ready, 1)
                    bn_finish(dve, 0)

                @block.tensor
                def _(pe):
                    def turn_group(s, h, g):
                        u = NG * s + g
                        a, b = GROUPS[g]
                        if g == 0:
                            pe.wait_ge(p_ready, s + 1)
                        wait(pe, t_out, u - 2)
                        for m in range(a, b):
                            t = pe.transpose(turn[g % 3][0:P, (m - a) * P:(m - a + 1) * P],
                                             v[h][:, m * P:(m + 1) * P], idt[0:P, 0:P])
                        t.then_inc(t_grp, 1)

                    def mul_group(j, q, h, g):
                        a, b = GROUPS[g]
                        pe.wait_ge(t_out, NG * (H3 * j + h) + g + 1)
                        if h == 0 and g == 0:
                            wait(pe, xc_ready, j - 1)
                        for m in range(a, b):
                            t = pe.matmul(acc[q][0:P, h * D3:(h + 1) * D3], pt[h % 2][:, m, :],
                                          HA[0:P, m, h * D3:(h + 1) * D3], start=(m == 0), stop=(m == T - 1))
                        t.then_inc(m_grp, 1)

                    for g in range(NG):
                        turn_group(0, 0, g)

                    def body(i):
                        for q in (0, 1):
                            j = 2 * i + q
                            final = isinstance(i, int) and j == T - 1
                            for h in range(H3):
                                nxt = not (final and h == H3 - 1)
                                for g in range(NG):
                                    if nxt:
                                        turn_group(H3 * j + h + 1, (h + 1) % H3, g)
                                    mul_group(j, q, h, g)
                                if isinstance(i, int) and j == 1 and h == 0:
                                    shift_matmul(pe, 0, xc[0][:, :])
                    pair_loop(pe, body, first=True, last=True)
                    bn_total(pe, 0)


        def elu_parts(ph):
            return [[sb(ph, f"{n_}{q}", [P, D]) for q in (0, 1)] for n_ in ("z", "e", "u")]

        with ExitStack() as ph:
            z, e, u = elu_parts(ph)
            xin = [sb(ph, f"xin{q}", [P, D]) for q in (0, 1)]
            xb = [sb(ph, f"xb{q}", [P, D]) for q in (0, 1)]
            xt = [sb(ph, f"xt{q}", [128, KT, P]) for q in (0, 1)]
            y = [sb(ph, f"y{k}", [P, D]) for k in (0, 1)]
            w_sb, bias = sb(ph, "w_sb", [128, KT, D]), sb(ph, "bias", [P, D])
            c_in, m_in = sem("mlp1_in"), sems("mlp1_x_in")
            xa_ready, xb_ready, z_ready, e_ready, u_ready = (sem(f"mlp1_{k}") for k in ("xa", "xb", "z", "e", "u"))
            tr, tr_out, mm_done = sem("mlp1_turned"), sem("mlp1_turned_out"), sem("mlp1_mm")
            with nc.Block() as block:
                @block.sync
                def _(sp):
                    sp.dma_start(w_sb[:, :, :], enc_w).then_inc(c_in, 16)
                    sp.dma_start(bias[:, :], enc_b.partition_broadcast(P)).then_inc(c_in, 16)

                    def body(i):
                        for q in (0, 1):
                            j = 2 * i + q
                            wait(sp, xa_ready, j - 1)
                            sp.dma_start(xin[q][:, :], xc_dram[j]).then_inc(m_in[q], 16)
                    pair_loop(sp, body, first=True)

                @block.vector
                def _(dve):
                    dve.wait_ge(c_in, 32)

                    def norm(i, q):
                        j = 2 * i + q
                        dve.wait_ge(m_in[q], 16 * (i + 1))
                        wait(dve, u_ready, j - 1)
                        wait(dve, tr, j - 1)
                        dve.tensor_tensor(xb[q][:, :], xin[q][:, :], a_bn[0][:, :], ALU.mult).then_inc(xa_ready, 1)
                        dve.wait_ge(xa_ready, j + 1)
                        dve.tensor_tensor(xb[q][:, :], xb[q][:, :], a_bn[1][:, :], ALU.add).then_inc(xb_ready, 1)

                    def linear(j, q):
                        dve.wait_ge(mm_done, j + 1)
                        wait(dve, e_ready, j - 1)
                        dve.tensor_tensor(z[q][:, :], pj[0:P, :], bias[:, :], ALU.add).then_inc(z_ready, 1)

                    def add(j, q):
                        dve.wait_ge(e_ready, j + 1)
                        dve.scalar_tensor_tensor(out=u[q][:, :], in0=e[q][:, :], scalar=1.0, in1=xb[q][:, :],
                                                 op0=ALU.min, op1=ALU.add).then_inc(u_ready, 1)
                        dve.wait_ge(u_ready, j + 1)
                        dve.scalar_tensor_tensor(out=HA[0:P, j, 0:D], in0=z[q][:, :], scalar=0.0, in1=u[q][:, :],
                                                 op0=ALU.max, op1=ALU.add).then_inc(xc_ready, 1)

                    def body(i):
                        for q in (0, 1):
                            j = 2 * i + q
                            norm(i, q)
                            if not (isinstance(i, int) and j == 0):
                                linear(j - 1, 1 - q)
                                add(j - 1, 1 - q)
                                if isinstance(i, int) and j == 1:
                                    shift_out(dve, 1)
                    pair_loop(dve, body, first=2)
                    linear(T - 1, 1)
                    add(T - 1, 1)
                    bn_finish(dve, 1)

                @block.tensor
                def _(pe):
                    pe.wait_ge(c_in, 32)

                    def turn_x(j, q):
                        pe.wait_ge(xb_ready, j + 1)
                        wait(pe, tr_out, j)
                        for k in range(KT):
                            t = pe.transpose(etp_view()[:, k, :], xb[q][:, k * 128:(k + 1) * 128], idt[0:P, 0:P])
                        t.then_inc(tr, 1)

                    def mul(j, q):
                        pe.wait_ge(tr_out, j + 1)
                        wait(pe, z_ready, j)
                        for k in range(KT):
                            t = pe.matmul(pj[0:P, :], xt[q][:, k, :], w_sb[:, k, :], start=(k == 0), stop=(k == KT - 1))
                        t.then_inc(mm_done, 1)

                    def body(i):
                        for q in (0, 1):
                            j = 2 * i + q
                            turn_x(j, q)
                            if not (isinstance(i, int) and j == 0):
                                mul(j - 1, 1 - q)
                                if isinstance(i, int) and j == 1:
                                    shift_matmul(pe, 1, HA[0:P, 0, 0:D])
                    pair_loop(pe, body, first=True)
                    mul(T - 1, 1)
                    bn_total(pe, 1)

                @block.scalar
                def _(act):
                    def expo(j, q):
                        act.wait_ge(z_ready, j + 1)
                        wait(act, u_ready, j - 1)
                        act.activation(e[q][:, :], z[q][:, :], ACT.Exp).then_inc(e_ready, 1)

                    def body(i):
                        for q in (0, 1):
                            j = 2 * i + q
                            act.wait_ge(tr, j + 1)
                            wait(act, mm_done, j - 1)
                            act.activation(xt[q][:, :, :], etp_view(), ACT.Copy).then_inc(tr_out, 1)
                            if not (isinstance(i, int) and j == 0):
                                expo(j - 1, 1 - q)
                    pair_loop(act, body, first=2)
                    expo(T - 1, 1)

                @block.gpsimd
                def _(pool):
                    sums_clear(pool, 1)
                    pool.wait_ge(shift_ready, 2)

                    def body(i):
                        for q in (0, 1):
                            j = 2 * i + q
                            if isinstance(i, int) and j == T - 1:
                                stats_tile(pool, T + j, y, HA[0:TAIL, j, 0:D], TAIL)
                            else:
                                stats_tile(pool, T + j, y, HA[0:P, j, 0:D], P)
                    pair_loop(pool, body, last=True)
                    bn_power(pool, 1)

        dec = ExitStack()
        XA = sb(dec, "XA", [P, T, D])
        with ExitStack() as ph:
            RING = 2 * H3
            w = [sb(ph, f"w{k}", [P, T, P]) for k in range(RING)]
            w_in = [sem(f"w_in{k}") for k in range(RING)]
            slot_done, att_out = sem("slot_done"), sem("att_out")
            with nc.Block() as block:
                @block.sync
                def _(sp):
                    def body(i):
                        for k in range(RING):
                            wait(sp, slot_done, RING * (i - 1) + k + 1)
                            sp.dma_start(w[k][:, :, :], weights[RING * i + k]).then_inc(w_in[k], 16)
                    pair_loop(sp, body, first=True)

                @block.tensor
                def _(pe):
                    def body(i):
                        for q in (0, 1):
                            for h in range(H3):
                                k = H3 * q + h
                                pe.wait_ge(w_in[k], 16 * (i + 1))
                                if h == 0:
                                    wait(pe, att_out, 2 * i + q - 1)
                                for m in range(T):
                                    t = pe.matmul(acc[q][0:P, h * D3:(h + 1) * D3], w[k][:, m, :],
                                                  HA[0:P, m, h * D3:(h + 1) * D3], start=(m == 0), stop=(m == T - 1))
                                t.then_inc(slot_done, 1)
                    pair_loop(pe, body, first=True)

                @block.vector
                def _(dve):
                    def body(i):
                        for q in (0, 1):
                            j = 2 * i + q
                            dve.wait_ge(slot_done, H3 * (j + 1))
                            dve.tensor_tensor(XA[:, j, :].rearrange("p (h e) -> p h e", e=D3),
                                              acc[q][0:P, :].rearrange("p (h e) -> p h e", e=D3),
                                              ri[:, j, :].unsqueeze(2).broadcast_to([P, H3, D3]),
                                              ALU.mult).then_inc(att_out, 1)
                    pair_loop(dve, body)


        with ExitStack() as ph:
            z, e, u = elu_parts(ph)
            e1 = [sb(ph, f"e1{q}", [P, D]) for q in (0, 1)]
            u1 = [sb(ph, f"u1{q}", [P, D]) for q in (0, 1)]
            yc = [sb(ph, f"yc{q}", [P, D]) for q in (0, 1)]
            xb = [sb(ph, f"xb{q}", [P, D]) for q in (0, 1)]
            xt = [sb(ph, f"xt{q}", [128, KT, P]) for q in (0, 1)]
            yt = [sb(ph, f"yt{q}", [128, KT, P]) for q in (0, 1)]
            y = [sb(ph, f"y{k}", [P, D]) for k in (0, 1)]
            w_sb, bias = sb(ph, "w_sb", [128, KT, D]), sb(ph, "bias", [P, D])
            wt_sb = sb(ph, "wt_sb", [128, H3, D3])
            c_in = sem("mlp2_in")
            xa_ready, xb_ready, z_ready, e_ready, u_ready = (sem(f"mlp2_{k}") for k in ("xa", "xb", "z", "e", "u"))
            e1_ready, u1_ready, yc_ready = (sem(f"mlp2_{k}") for k in ("e1", "u1", "yc"))
            tr, tr_out, mm_done = sem("mlp2_turned"), sem("mlp2_turned_out"), sem("mlp2_mm")
            tr1, tr1_out, mm1_done = sem("mlp2_turned1"), sem("mlp2_turned1_out"), sem("mlp2_mm1")
            tp1, pj1 = bank[2], bank[3]

            def tp1_view():
                return tp1[:, 0:KT * P].rearrange("p (k n) -> p k n", k=KT)

            with nc.Block() as block:
                @block.sync
                def _(sp):
                    sp.dma_start(w_sb[:, :, :], dec_w).then_inc(c_in, 16)
                    sp.dma_start(bias[:, :], dec_b.partition_broadcast(P)).then_inc(c_in, 16)
                    sp.dma_start(wt_sb[:, :, :], w3t.rearrange("p (h d) -> p h d", h=H3)).then_inc(c_in, 16)

                @block.vector
                def _(dve):
                    dve.wait_ge(c_in, 48)

                    def norm(i, q):
                        j = 2 * i + q
                        wait(dve, tr, j - 1)
                        dve.tensor_tensor(xb[q][:, :], XA[:, j, :], a_bn[0][:, :], ALU.mult).then_inc(xa_ready, 1)
                        dve.wait_ge(xa_ready, j + 1)
                        dve.scalar_tensor_tensor(out=xb[q][:, :], in0=a_bn[1][:, :], scalar=has_edge[:, bass.ds(j, 1)],
                                                 in1=xb[q][:, :], op0=ALU.mult, op1=ALU.add).then_inc(xb_ready, 1)

                    def first_elu(j, q):
                        dve.wait_ge(e1_ready, j + 1)
                        dve.tensor_scalar(u1[q][:, :], e1[q][:, :], 1.0, -1.0, ALU.min, ALU.add).then_inc(u1_ready, 1)
                        dve.wait_ge(u1_ready, j + 1)
                        wait(dve, tr1, j - 1)
                        dve.scalar_tensor_tensor(out=yc[q][:, :], in0=pj1[0:P, :], scalar=0.0, in1=u1[q][:, :],
                                                 op0=ALU.max, op1=ALU.add).then_inc(yc_ready, 1)

                    def linear(j, q):
                        dve.wait_ge(mm_done, j + 1)
                        wait(dve, e_ready, j - 1)
                        dve.tensor_tensor(z[q][:, :], pj[0:P, :], bias[:, :], ALU.add).then_inc(z_ready, 1)

                    def add(j, q):
                        dve.wait_ge(e_ready, j + 1)
                        dve.scalar_tensor_tensor(out=u[q][:, :], in0=e[q][:, :], scalar=1.0, in1=yc[q][:, :],
                                                 op0=ALU.min, op1=ALU.add).then_inc(u_ready, 1)
                        dve.wait_ge(u_ready, j + 1)
                        dve.scalar_tensor_tensor(out=HA[0:P, j, 0:D], in0=z[q][:, :], scalar=0.0, in1=u[q][:, :],
                                                 op0=ALU.max, op1=ALU.add).then_inc(xc_ready, 1)

                    def body(i):
                        for q in (0, 1):
                            j = 2 * i + q
                            norm(i, q)
                            if not (isinstance(i, int) and j == 0):
                                linear(j - 1, 1 - q)
                                add(j - 1, 1 - q)
                                if isinstance(i, int) and j == 1:
                                    shift_out(dve, 2)
                            first_elu(j, q)
                    pair_loop(dve, body, first=2)
                    linear(T - 1, 1)
                    add(T - 1, 1)
                    bn_finish(dve, 2)

                @block.tensor
                def _(pe):
                    pe.wait_ge(c_in, 48)

                    def body(i):
                        for q in (0, 1):
                            j = 2 * i + q
                            pe.wait_ge(xb_ready, j + 1)
                            wait(pe, tr_out, j)
                            for k in range(KT):
                                t = pe.transpose(etp_view()[:, k, :], xb[q][:, k * 128:(k + 1) * 128], idt[0:P, 0:P])
                            t.then_inc(tr, 1)
                            pe.wait_ge(tr_out, j + 1)
                            wait(pe, yc_ready, j)
                            for h in range(H3):
                                t = pe.matmul(pj1[0:P, h * D3:(h + 1) * D3], xt[q][:, h, :], wt_sb[:, h, :],
                                              start=True, stop=True)
                            t.then_inc(mm1_done, 1)
                            if isinstance(i, int) and j == 1:
                                shift_matmul(pe, 2, HA[0:P, 0, 0:D])
                            pe.wait_ge(yc_ready, j + 1)
                            wait(pe, tr1_out, j)
                            for k in range(KT):
                                t = pe.transpose(tp1_view()[:, k, :], yc[q][:, k * 128:(k + 1) * 128], idt[0:P, 0:P])
                            t.then_inc(tr1, 1)
                            pe.wait_ge(tr1_out, j + 1)
                            wait(pe, z_ready, j)
                            for k in range(KT):
                                t = pe.matmul(pj[0:P, :], yt[q][:, k, :], w_sb[:, k, :], start=(k == 0),
                                              stop=(k == KT - 1))
                            t.then_inc(mm_done, 1)
                    pair_loop(pe, body, first=True)
                    bn_total(pe, 2)

                @block.scalar
                def _(act):
                    def expo(j, q):
                        act.wait_ge(z_ready, j + 1)
                        wait(act, u_ready, j - 1)
                        act.activation(e[q][:, :], z[q][:, :], ACT.Exp).then_inc(e_ready, 1)

                    def body(i):
                        for q in (0, 1):
                            j = 2 * i + q
                            act.wait_ge(tr, j + 1)
                            wait(act, mm1_done, j - 1)
                            act.activation(xt[q][:, :, :], etp_view(), ACT.Copy).then_inc(tr_out, 1)
                            if not (isinstance(i, int) and j == 0):
                                expo(j - 1, 1 - q)
                            act.wait_ge(mm1_done, j + 1)
                            wait(act, u1_ready, j - 1)
                            act.activation(e1[q][:, :], pj1[0:P, :], ACT.Exp).then_inc(e1_ready, 1)
                            act.wait_ge(tr1, j + 1)
                            wait(act, mm_done, j - 1)
                            act.activation(yt[q][:, :, :], tp1_view(), ACT.Copy).then_inc(tr1_out, 1)
                    pair_loop(act, body, first=2)
                    expo(T - 1, 1)

                @block.gpsimd
                def _(pool):
                    sums_clear(pool, 2)
                    pool.wait_ge(shift_ready, 3)

                    def body(i):
                        for q in (0, 1):
                            j = 2 * i + q
                            if isinstance(i, int) and j == T - 1:
                                stats_tile(pool, 2 * T + j, y, HA[0:TAIL, j, 0:D], TAIL)
                            else:
                                stats_tile(pool, 2 * T + j, y, HA[0:P, j, 0:D], P)
                    pair_loop(pool, body, last=True)
                    bn_power(pool, 2)

        dec.close()

        with ExitStack() as ph:
            R, xn, st, xin, xt, bias, w_sb = norm_buffers(ph)
            m_in = sems("last_x_in")
            xa_ready = sem("last_xa")
            with nc.Block() as block:
                @block.sync
                def _(sp):
                    def body(i):
                        for q in (0, 1):
                            j = 2 * i + q
                            wait(sp, r_full, 3 * T + j - 1)
                            sp.dma_start(xin[q][:, :], xs[2][j]).then_inc(m_in[q], 16)
                    pair_loop(sp, body, first=True)

                @block.vector
                def _(dve):
                    def half_sum(j, q):
                        dve.tensor_tensor(R[q][:, :], HA[0:P, j, 0:D], a_bn[0][:, :], ALU.mult).then_inc(xa_ready, 1)

                    def body(i):
                        for q in (0, 1):
                            j = 2 * i + q
                            n = 3 * T + j
                            half_sum(j, q)
                            dve.wait_ge(xa_ready, j + 1)
                            dve.tensor_tensor(R[q][:, :], R[q][:, :], a_bn[1][:, :], ALU.add).then_inc(r_half, 1)
                            dve.wait_ge(r_half, 2 * T + j + 1)
                            dve.wait_ge(m_in[q], 16 * (i + 1))
                            dve.tensor_tensor(R[q][:, :], R[q][:, :], xin[q][:, :], ALU.add).then_inc(r_full, 1)
                            ln_tile(dve, n, q, R, st, xn)
                            dve.wait_ge(xn_stored[q], 16 * (3 * PAIRS + i))
                            ln_write(dve, n, q, R, st, xn[q][:, :])
                    pair_loop(dve, body)

                @block.gpsimd
                def _(pool):
                    def body(i):
                        for q in (0, 1):
                            norm_store(pool, i, q, 3 * T + 2 * i + q, out, st, xn)
                    pair_loop(pool, body)
                    for q in (0, 1):
                        pool.wait_ge(xn_stored[q], 16 * 4 * PAIRS)




def _p(a):
    import numpy as np
    return np.pad(a, [(0, NP - N if s == N else 0) for s in a.shape])


def layout(inputs):
    import numpy as np
    g = {k: np.asarray(v) for k, v in inputs.items()}

    def blocks(w):
        return np.ascontiguousarray(w.reshape(KT, 128, -1).transpose(1, 0, 2))

    def columns(v):
        return np.ascontiguousarray(v.reshape(KT, 128).T)

    adj = _p(g["adj"])
    adj_t = np.ascontiguousarray(adj.T)
    L3 = "L3_gnn_"
    return {
        "x": _p(g["x"]).reshape(T, P, D),
        "adj_rows": adj.reshape(T, P, NP),
        "adj_cols": adj_t.reshape(T, P, NP),
        "adj_tiles": np.ascontiguousarray(adj.reshape(T, P, T, P).transpose(0, 3, 2, 1)),
        "ident": np.eye(128, dtype=np.float32),
        "w0": blocks(g["L0_gnn_kernels"].transpose(1, 0, 2).reshape(D, D)),
        "a0_self": g["L0_gnn_attn_self"].reshape(D),
        "a0_neigh": g["L0_gnn_attn_neigh"].reshape(D),
        "b0": g["L0_gnn_biases"].reshape(D),
        "w1": blocks(g["L1_gnn_W"].transpose(1, 0, 2).reshape(D, D)),
        "b1": g["L1_gnn_b"].reshape(D),
        "w2a": blocks(g["L2_gnn_W"][:D]),
        "w2b": blocks(g["L2_gnn_W"][D:]),
        "a2_w": g["L2_gnn_a_w"],
        "a2_b": g["L2_gnn_a_b"].reshape(1),
        "fc_w": blocks(g["L2_gnn_fc_w"]),
        "fc_b": g["L2_gnn_fc_b"],
        "w3": np.ascontiguousarray(g[L3 + "W"].transpose(1, 0, 2)).reshape(D3, D),
        "w3t": np.ascontiguousarray(g[L3 + "W"].transpose(2, 0, 1)).reshape(D3, D),
        "v3a": np.ascontiguousarray(g[L3 + "V"][:, 0, :, 0]).reshape(D),
        "v3b": np.ascontiguousarray(g[L3 + "V"][:, 1, :, 0]).reshape(D),
        "enc_w": blocks(g[L3 + "enc_mlp_W"].T),
        "enc_b": g[L3 + "enc_mlp_b"],
        "dec_w": blocks(g[L3 + "dec_mlp_W"].T),
        "dec_b": g[L3 + "dec_mlp_b"],
        "g_bn": np.stack([columns(g[L3 + k]) for k in ("enc_bn_gamma", "enc_mlp_bn_gamma", "dec_mlp_bn_gamma")], 1),
        "b_bn": np.stack([columns(g[L3 + k]) for k in ("enc_bn_beta", "enc_mlp_bn_beta", "dec_mlp_bn_beta")], 1),
    }


def kernel(**inputs):
    import numpy as _np
    import concourse.bacc as _bacc
    from concourse import mybir as _mybir
    from concourse.bass_utils import run_bass_kernel_spmd as _run

    nc = _bacc.Bacc("TRN2", target_bir_lowering=False, num_devices=1)
    arrays = layout(inputs)
    aps = {k: nc.dram_tensor(f"in_{k}", a.shape, _mybir.dt.from_np(a.dtype), kind="ExternalInput").ap()
           for k, a in arrays.items()}
    out = nc.dram_tensor("out_0", (T, P, D), _mybir.dt.float32, kind="ExternalOutput").ap()
    build(nc, **aps, out=out)
    r = _run(nc, [{f"in_{k}": a for k, a in arrays.items()}], core_ids=[0])
    return _np.ascontiguousarray(r.results[0]["out_0"].reshape(NP, D)[:N])
```

```python
import concourse.bass as bass
from concourse import mybir
from contextlib import ExitStack

FP32 = mybir.dt.float32
F32R = mybir.dt.float32r
U8 = mybir.dt.uint8
ALU = mybir.AluOpType
ACT = mybir.ActivationFunctionType
AX = mybir.AxisListType

N = 2708
D = 512
T = 22
P = 124
NP = T * P
TAIL = N - (T - 1) * P
PAIRS = T // 2
KT = D // 128
H0, F0 = 8, 64
FW = F0 + 1
H3, D3 = 4, 128
CH = 2
CT = T // CH
CW = CT * P
TA = 6
GROUPS = [(a, min(a + 4, T)) for a in range(0, T, 4)]
NG = len(GROUPS)
EPS0 = 2.220446049250313e-16
LN_EPS = 1e-5
BN_EPS = 1e-6
HT = T // 2
FAR = 255.0
NEG = -9e15
LOW = -3e38
SQ_ON_ACT = [m % 5 in (0, 2, 4) for m in range(T)]


def wait(eng, sem, value):
    if isinstance(value, int) and value <= 0:
        return
    eng.wait_ge(sem, value)


def count(eng, value):
    return value if isinstance(value, int) else eng.to_reg(value)


def carry(eng, settled, value):
    eng.wait_ge(settled, value)


def pair_loop(eng, body, first=0, last=False):
    lo, hi = int(first), PAIRS - int(last)
    for i in range(lo):
        body(i)
    with eng.Fori(lo, hi) as i:
        body(i)
    if last:
        body(PAIRS - 1)


def build(nc, x, adj_rows, adj_cols, adj_tiles, ident, w0, a0_self, a0_neigh, b0, w1, b1, w2a, w2b, a2_w, a2_b,
          fc_w, fc_b, w3, w3t, v3a, v3b, enc_w, enc_b, dec_w, dec_b, g_bn, b_bn, out, dbg=None):
    top = ExitStack()
    kind = "ExternalOutput" if dbg else "Internal"

    def scratch(name, shape):
        return nc.dram_tensor(name, shape, FP32, kind=kind).ap()

    xs = [scratch(f"x_after_{k}", [T, P, D]) for k in range(3)]
    rows0 = scratch("score_rows_0", [H0, NP])
    rows2 = scratch("score_rows_2", [1, NP])
    rows3 = scratch("score_rows_3", [H3, NP])
    xw_dram = scratch("features_3", [T, P, D])
    xc_dram = scratch("attended", [T, P, D])

    def sem(name):
        return top.enter_context(nc.semaphore(name))

    def sems(name, n=2):
        return [sem(f"{name}{k}") for k in range(n)]

    names = set()

    def sb(stack, name, shape, dt=FP32):
        k = 0
        while f"{name}_{k}" in names:
            k += 1
        names.add(f"{name}_{k}")
        return stack.enter_context(nc.sbuf_tensor(f"{name}_{k}", shape, dt))

    with top:
        idt = sb(top, "idt", [128, 128])
        ones = sb(top, "ones", [128, 128])
        u0s, u0n = sb(top, "u0s", [128, KT, H0]), sb(top, "u0n", [128, KT, H0])
        u2s, u2n = sb(top, "u2s", [128, KT, 1]), sb(top, "u2n", [128, KT, 1])
        u3s, u3n = sb(top, "u3s", [128, KT, H3]), sb(top, "u3n", [128, KT, H3])
        neg_t = sb(top, "neg_t", [128, T, H0])
        s1 = sb(top, "s1", [128, T])
        f1 = sb(top, "f1", [128, T, H3])
        half = sb(top, "half", [128, 1])
        ab2 = sb(top, "ab2", [128, 1])
        bank = [top.enter_context(nc.psum_tensor(f"bank{k}", [128, 512], FP32)) for k in range(8)]
        acc = bank[0:2]
        turn = bank[2:5]
        etp, pj, sc = bank[5], bank[6], bank[7]

        set_const = sem("set_const")
        turned, turned_out = sem("turned"), sem("turned_out")
        proj_mm, proj_out = sem("proj_mm"), sem("proj_out")
        score_mm, score_out = sem("score_mm"), sem("score_out")
        x_in = sems("x_in")
        r_half, r_full = sem("r_half"), sem("r_full")
        ln_stats, ln_mean, ln_var, ln_rstd, ln_done = (sem(f"ln_{k}") for k in ("stats", "mean", "var", "rstd", "done"))
        xn_stored = sems("xn_stored")
        row_stored = sems("row_stored")

        def etp_view(n=P):
            return etp[:, 0:KT * n].rearrange("p (k n) -> p k n", k=KT)

        def turn_tile(pe, n, src):
            wait(pe, turned_out, n)
            for k in range(KT):
                t = pe.transpose(etp_view()[:, k, :], src[0:P, k * 128:(k + 1) * 128], idt[0:P, 0:P])
            t.then_inc(turned, 1)

        def keep_turned(act, n, xt):
            act.wait_ge(turned, n + 1)
            wait(act, proj_mm, n - 1)
            act.activation(xt[:, :, :], etp_view(), ACT.Copy).then_inc(turned_out, 1)

        def project(pe, n, xt, w, u_col, u_row, heads, blocked=False):
            pe.wait_ge(turned_out, n + 1)
            if heads:
                wait(pe, score_out, score_base[0] + n)
                for k in range(KT):
                    pe.matmul(sc[0:P, 0:heads], xt[:, k, :], u_col[:, k, :], start=(k == 0), stop=(k == KT - 1))
                for k in range(KT):
                    t = pe.matmul(sc[0:heads, 16:16 + P], u_row[:, k, :], xt[:, k, :],
                                  start=(k == 0), stop=(k == KT - 1))
                t.then_inc(score_mm, 1)
            wait(pe, proj_out, n)
            for k in range(KT):
                if blocked:
                    t = pe.matmul(pj[0:P, k * D3:(k + 1) * D3], xt[:, k, :], w[:, k, :], start=True, stop=True)
                else:
                    t = pe.matmul(pj[0:P, :], xt[:, k, :], w[:, k, :], start=(k == 0), stop=(k == KT - 1))
            t.then_inc(proj_mm, 1)

        score_base = [0]

        def ln_tile(dve, n, q, R, st, xn):
            dve.wait_ge(r_full, n + 1)
            dve.bn_stats(st[q][:, 0:6], R[q][:, :]).then_inc(ln_stats, 1)
            carry(dve, set_const, 1)
            dve.wait_ge(ln_stats, n + 1)
            dve.bn_aggr(st[q][:, 6:8], st[q][:, 0:6]).then_inc(ln_mean, 1)
            dve.wait_ge(ln_mean, n + 1)
            dve.tensor_scalar(st[q][:, 8:9], st[q][:, 7:8], LN_EPS, None, ALU.add).then_inc(ln_var, 1)
            dve.wait_ge(ln_rstd, n + 1)

        def ln_write(dve, n, q, R, st, dst):
            dve.tensor_scalar(dst, R[q][:, :], st[q][:, 6:7], st[q][:, 9:10], ALU.subtract, ALU.mult)\
               .then_inc(ln_done, 1)

        def ln_power(pool, n, q, st):
            pool.wait_ge(ln_var, n + 1)
            pool.tensor_tensor(st[q][:, 9:10], st[q][:, 8:9], half[0:P, :], ALU.pow).then_inc(ln_rstd, 1)

        L0 = ExitStack()
        HB = sb(L0, "HB", [128, T, D])
        features_0 = ExitStack()
        HA = sb(features_0, "HA", [128, T, H0 * FW])
        with ExitStack() as ph:
            msk_stack = ExitStack()
            msk = sb(msk_stack, "msk", [P, T, NP], U8)
            w0_sb = sb(ph, "w0_sb", [128, KT, D])
            xin = [sb(ph, f"xin{q}", [P, D]) for q in (0, 1)]
            xt = [sb(ph, f"xt{q}", [128, KT, P]) for q in (0, 1)]
            srow = [sb(ph, f"srow{q}", [H0, P]) for q in (0, 1)]
            al = [sb(ph, f"al{q}", [P, NP]) for q in (0, 1)]
            vec = HB[:, 16:18, :]
            tmp = HB[:, 0:4, :]
            wld = HB[:, 4:16, :]
            w_in, vec_in, u_in = sem("w0_in"), sem("vec0_in"), sem("fold_in")
            adj_in, mask_done = sems("mask_adj_in"), sem("mask_done")
            fold_mul, fold_sum = sem("fold_mul"), sem("fold_sum")
            vecs = [HB[:, 16 + k, :] for k in range(5)]
            with nc.Block() as block:
                @block.sync
                def _(sp):
                    sp.dma_start(w0_sb[:, :, :], w0).then_inc(w_in, 16)
                    sp.dma_start(vecs[0], a0_self.partition_broadcast(128)).then_inc(vec_in, 16)
                    sp.dma_start(vecs[1], a0_neigh.partition_broadcast(128)).then_inc(vec_in, 16)
                    sp.dma_start(idt[:, :], ident).then_inc(vec_in, 16)

                    def body(i):
                        for q in (0, 1):
                            j = 2 * i + q
                            wait(sp, turned, j - 1)
                            sp.dma_start(xin[q][:, :], x[j]).then_inc(x_in[q], 16)
                            wait(sp, mask_done, j - 1)
                            sp.dma_start(al[q][:, :], adj_cols[j]).then_inc(adj_in[q], 16)
                    pair_loop(sp, body, first=True)

                @block.gpsimd
                def _(pool):
                    pool.dma_start(vecs[2], a2_w.partition_broadcast(128)).then_inc(u_in, 16)
                    pool.dma_start(vecs[3], v3a.partition_broadcast(128)).then_inc(u_in, 16)
                    pool.dma_start(vecs[4], v3b.partition_broadcast(128)).then_inc(u_in, 16)
                    pool.dma_start(wld[:, 0:4, :], w2a).then_inc(u_in, 16)
                    pool.dma_start(wld[:, 4:8, :], w2b).then_inc(u_in, 16)
                    pool.dma_start(wld[:, 8, :], w3).then_inc(u_in, 16)
                    pool.dma_start(ab2[:, :], a2_b.partition_broadcast(128)).then_inc(u_in, 16)

                    def body(i):
                        for q in (0, 1):
                            pool.wait_ge(score_out, 2 * (2 * i + q) + 2)
                            pool.dma_start(rows0[:, bass.ds((2 * i + q) * P, P)], srow[q][:, :])\
                                .then_inc(row_stored[q], 16)
                    pair_loop(pool, body)
                    for q in (0, 1):
                        pool.wait_ge(row_stored[q], 16 * PAIRS)
                    pool.wait_ge(u_in, 7 * 16)

                @block.tensor
                def _(pe):
                    pe.wait_ge(vec_in, 48)
                    pe.wait_ge(w_in, 16)

                    def scores(n, q):
                        pe.wait_ge(turned_out, n + 1)
                        wait(pe, score_out, 2 * n)
                        if isinstance(n, int) and n == 0:
                            pe.wait_ge(fold_sum, 2)
                        for k in range(KT):
                            pe.matmul(sc[0:P, 0:H0], xt[q][:, k, :], u0n[:, k, :], start=(k == 0), stop=(k == KT - 1))
                        for k in range(KT):
                            t = pe.matmul(sc[0:H0, 16:16 + P], u0s[:, k, :], xt[q][:, k, :],
                                          start=(k == 0), stop=(k == KT - 1))
                        t.then_inc(score_mm, 1)
                        project(pe, n, xt[q], w0_sb, None, None, 0)

                    def body(i):
                        for q in (0, 1):
                            j = 2 * i + q
                            pe.wait_ge(x_in[q], 16 * (i + 1))
                            turn_tile(pe, j, xin[q])
                            if not (isinstance(i, int) and j == 0):
                                scores(j - 1, 1 - q)
                    pair_loop(pe, body, first=True)
                    scores(T - 1, 1)

                @block.scalar
                def _(act):
                    def scores_out(n, q, wait_row):
                        act.wait_ge(score_mm, n + 1)
                        act.activation(neg_t[0:P, n, :], sc[0:P, 0:H0], ACT.Copy, scale=-1.0).then_inc(score_out, 1)
                        wait(act, row_stored[q], wait_row)
                        act.activation(srow[q][:, :], sc[0:H0, 16:16 + P], ACT.Copy).then_inc(score_out, 1)

                    def body(i):
                        for q in (0, 1):
                            j = 2 * i + q
                            keep_turned(act, j, xt[q])
                            if not (isinstance(i, int) and j == 0):
                                scores_out(j - 1, 1 - q, 16 * (i if q else i - 1))
                    pair_loop(act, body, first=2)
                    scores_out(T - 1, 1, 16 * (PAIRS - 1))

                @block.vector
                def _(dve):
                    dve.memset(half[:, :], -0.5).then_inc(set_const, 1)
                    dve.memset(ones[:, :], 1.0).then_inc(set_const, 1)
                    dve.memset(u3s[:, :, :], 0.0).then_inc(set_const, 1)
                    dve.memset(u3n[:, :, :], 0.0).then_inc(set_const, 1)
                    for h in range(H0):
                        dve.memset(HA[:, :, h * FW + F0], 1.0).then_inc(set_const, 1)
                    done = [0, 0]

                    def fold(weights, vector, parts, width, dst, stock):
                        wait(dve, fold_sum, done[1])
                        for k in range(stock):
                            dve.tensor_tensor(tmp[:, k, :], weights(k), vector, ALU.mult).then_inc(fold_mul, 1)
                            done[0] += 1
                        dve.wait_ge(fold_mul, done[0])
                        dve.tensor_reduce(dst, tmp[:, 0:stock, :].rearrange("p k (h f) -> p (k h) f", f=width),
                                          AX.X, ALU.add).then_inc(fold_sum, 1)
                        done[1] += 1

                    dve.wait_ge(w_in, 16)
                    dve.wait_ge(vec_in, 48)
                    fold(lambda k: w0_sb[:, k, :], vecs[1], H0, F0, u0n[:, :, :].rearrange("p k h -> p (k h)"), KT)
                    fold(lambda k: w0_sb[:, k, :], vecs[0], H0, F0, u0s[:, :, :].rearrange("p k h -> p (k h)"), KT)
                    dve.wait_ge(u_in, 7 * 16)
                    dve.wait_ge(set_const, 4)
                    fold(lambda k: wld[:, k, :], vecs[2], 1, D, u2s[:, :, 0], KT)
                    fold(lambda k: wld[:, 4 + k, :], vecs[2], 1, D, u2n[:, :, 0], KT)
                    fold(lambda k: wld[:, 8, :], vecs[3], H3, D3,
                         u3s[:, :, :].rearrange("p k h -> p (k h)")[:, 0:KT * H3:H3 + 1], 1)
                    fold(lambda k: wld[:, 8, :], vecs[4], H3, D3,
                         u3n[:, :, :].rearrange("p k h -> p (k h)")[:, 0:KT * H3:H3 + 1], 1)
                    dve.wait_ge(set_const, 4 + H0)

                    def feats_out(n):
                        dve.wait_ge(proj_mm, n + 1)
                        dve.tensor_copy(HA[0:P, n, :].rearrange("p (h w) -> p h w", w=FW)[:, :, 0:F0],
                                        pj[0:P, :].rearrange("p (h f) -> p h f", f=F0)).then_inc(proj_out, 1)

                    def body(i):
                        for q in (0, 1):
                            j = 2 * i + q
                            dve.wait_ge(adj_in[q], 16 * (i + 1))
                            dve.tensor_scalar(msk[:, j, :], al[q][:, :], 0.0, FAR, ALU.is_le, ALU.mult)\
                               .then_inc(mask_done, 1)
                            if not (isinstance(i, int) and j == 0):
                                feats_out(j - 1)
                    pair_loop(dve, body, first=True)
                    feats_out(T - 1)

        with ExitStack() as ph:
            sB = [sb(ph, f"sB{q}", [P, CW]) for q in (0, 1)]
            dist = [sb(ph, f"dist{k}", [P, CW]) for k in range(4)]
            hf = [sb(ph, f"hf{q}", [P, T, FW]) for q in (0, 1)]
            hf_ready = sem("hf_ready")
            sums = sb(ph, "sums", [FW, CW])
            den = sb(ph, "den", [P, CT])
            rden = sb(ph, "rden", [P, CT])
            s_in = sems("s_in")
            d_ready, sq_act, sq_dve, p_ready, pv_done = (sem(k) for k in ("d_ready", "sq_act", "sq_dve", "p_ready", "pv_done"))
            sums_out, sums_turned = sem("sums_out"), sem("sums_turned")
            den_ready, rden_ready, head_out = sem("den_ready"), sem("rden_ready"), sem("head_out")
            n_act = sum(SQ_ON_ACT)
            n_dve = T - n_act

            EVAC_AT, TURN_AT, RESULT_AT = (3, 4, 5), 6, 12
            PARTS = [(a, min(a + 4, CT)) for a in range(0, CT, 4)]

            def sums_bank(hh, k):
                return bank[3 * hh + k]

            def group(c, hp, hh):
                return c * H0 + hp * 2 + hh

            def head_loop(eng, body, c, first):
                if first:
                    body(0)
                with eng.Fori(int(first), H0 // 2) as hp:
                    body(hp)

            with nc.Block() as block:
                @block.sync
                def _(sp):
                    for c in range(CH):
                        def body(hp):
                            for hh in (0, 1):
                                wait(sp, d_ready, (group(c, hp, hh) - 1) * T)
                                sp.dma_start(sB[hh][:, :],
                                             rows0[hp * 2 + hh, c * CW:(c + 1) * CW].partition_broadcast(P))\
                                  .then_inc(s_in[hh], 16)
                        head_loop(sp, body, c, True)

                @block.vector
                def _(dve):
                    def head_result(c, h, g):
                        a, b = bank[6], bank[7]
                        va = a[0:P, 0:TA * FW].rearrange("p (t w) -> p t w", w=FW)
                        vb = b[0:P, 0:(CT - TA) * FW].rearrange("p (t w) -> p t w", w=FW)
                        dve.wait_ge(sums_turned, g + 1)
                        dve.tensor_scalar(den[:, 0:TA], va[:, :, F0], EPS0, None, ALU.add).then_inc(den_ready, 1)
                        dve.tensor_scalar(den[:, TA:CT], vb[:, :, F0], EPS0, None, ALU.add).then_inc(den_ready, 1)
                        dve.wait_ge(den_ready, 2 * (g + 1))
                        dve.reciprocal(rden[:, :], den[:, :]).then_inc(rden_ready, 1)
                        dve.wait_ge(rden_ready, g + 1)
                        for v, lo, hi in ((va, 0, TA), (vb, TA, CT)):
                            dve.tensor_tensor(HB[0:P, c * CT + lo:c * CT + hi, bass.ds(h * F0, F0)], v[:, :, 0:F0],
                                              rden[:, lo:hi].unsqueeze(2).broadcast_to([P, hi - lo, F0]),
                                              ALU.mult).then_inc(head_out, 1)

                    for c in range(CH):
                        def body(hp):
                            for hh in (0, 1):
                                g = group(c, hp, hh)
                                dve.wait_ge(s_in[hh], 16 * (c * (H0 // 2) + hp + 1))
                                late = None
                                for m in range(T):
                                    s = g * T + m
                                    d = dist[(hh * T + m) % 4]
                                    wait(dve, pv_done, s - 3)
                                    if SQ_ON_ACT[m]:
                                        dve.tensor_tensor(d[:, :], msk[:, m, c * CW:(c + 1) * CW], sB[hh][:, :],
                                                          ALU.add).then_inc(d_ready, 1)
                                    else:
                                        dve.scalar_tensor_tensor(
                                            out=d[:, :], in0=msk[:, m, c * CW:(c + 1) * CW],
                                            scalar=neg_t[0:P, m, bass.ds(hp * 2 + hh, 1)], in1=sB[hh][:, :],
                                            op0=ALU.add, op1=ALU.add).then_inc(d_ready, 1)
                                    if late is not None:
                                        dve.wait_ge(d_ready, late[1] + 1)
                                        dve.tensor_tensor(late[0][:, :], late[0][:, :], late[0][:, :], ALU.mult)\
                                           .then_inc(sq_dve, 1)
                                        late = None
                                    if not SQ_ON_ACT[m]:
                                        late = (d, s)
                                    if m == RESULT_AT and not (isinstance(hp, int) and hp == 0 and c == 0 and hh == 0):
                                        if hh == 1:
                                            head_result(c, hp * 2, g - 1)
                                        elif isinstance(hp, int) and hp == 0:
                                            head_result(c - 1, H0 - 1, g - 1)
                                        else:
                                            head_result(c, hp * 2 - 1, g - 1)
                                if late is not None:
                                    dve.wait_ge(d_ready, late[1] + 1)
                                    dve.tensor_tensor(late[0][:, :], late[0][:, :], late[0][:, :], ALU.mult)\
                                       .then_inc(sq_dve, 1)
                        head_loop(dve, body, c, True)
                    head_result(CH - 1, H0 - 1, CH * H0 - 1)

                @block.gpsimd
                def _(pool):
                    for c in range(CH):
                        def body(hp):
                            for hh in (0, 1):
                                g = group(c, hp, hh)
                                wait(pool, pv_done, (g - 1) * T)
                                pool.tensor_copy(hf[hh][:, :, :], HA[0:P, :, bass.ds((hp * 2 + hh) * FW, FW)])\
                                    .then_inc(hf_ready, 1)
                        head_loop(pool, body, c, True)

                @block.scalar
                def _(act):
                    def evacuate(g, hh, k):
                        a, b = PARTS[k]
                        if k == 0:
                            act.wait_ge(pv_done, (g + 1) * T)
                            wait(act, sums_turned, g)
                        act.activation(sums[:, a * P:b * P], sums_bank(hh, k)[0:FW, 0:(b - a) * P], ACT.Copy)\
                           .then_inc(sums_out, 1)

                    for c in range(CH):
                        def body(hp):
                            for hh in (0, 1):
                                g = group(c, hp, hh)
                                first = isinstance(g, int) and g == 0

                                def square(m):
                                    if SQ_ON_ACT[m]:
                                        d = dist[(hh * T + m) % 4]
                                        act.wait_ge(d_ready, g * T + m + 1)
                                        act.activation(d[:, :], d[:, :], ACT.Square,
                                                       bias=neg_t[0:P, m, bass.ds(hp * 2 + hh, 1)]).then_inc(sq_act, 1)

                                def expo(m):
                                    d = dist[(hh * T + m) % 4]
                                    if SQ_ON_ACT[m]:
                                        act.wait_ge(sq_act, g * n_act + sum(SQ_ON_ACT[:m + 1]))
                                    else:
                                        act.wait_ge(sq_dve, g * n_dve + (m + 1 - sum(SQ_ON_ACT[:m + 1])))
                                    act.activation(d[:, :], d[:, :], ACT.Exp, scale=-1.0).then_inc(p_ready, 1)

                                square(0)
                                for m in range(T):
                                    if m + 1 < T:
                                        square(m + 1)
                                    expo(m)
                                    if m in EVAC_AT and not first:
                                        evacuate(g - 1, 1 - hh, EVAC_AT.index(m))
                        head_loop(act, body, c, c == 0)
                    for k in range(len(PARTS)):
                        evacuate(CH * H0 - 1, 1, k)

                @block.tensor
                def _(pe):
                    def turn_sums(g):
                        pe.wait_ge(sums_out, len(PARTS) * (g + 1))
                        wait(pe, head_out, 2 * g)
                        for t in range(CT):
                            o = (t - TA if t >= TA else t) * FW
                            mm = pe.transpose(bank[6 + (t >= TA)][0:P, o:o + FW], sums[:, t * P:(t + 1) * P],
                                              idt[0:FW, 0:FW])
                        mm.then_inc(sums_turned, 1)

                    for c in range(CH):
                        def body(hp):
                            for hh in (0, 1):
                                g = group(c, hp, hh)
                                for m in range(T):
                                    if m == 0:
                                        pe.wait_ge(hf_ready, g + 1)
                                        wait(pe, sums_out, len(PARTS) * (g - 1))
                                    pe.wait_ge(p_ready, g * T + m + 1)
                                    d = dist[(hh * T + m) % 4]
                                    for k, (a, b) in enumerate(PARTS):
                                        mm = pe.matmul(sums_bank(hh, k)[0:FW, 0:(b - a) * P], hf[hh][:, m, :],
                                                       d[:, a * P:b * P], start=(m == 0), stop=(m == T - 1))
                                    mm.then_inc(pv_done, 1)
                                    if m == TURN_AT and not (isinstance(g, int) and g == 0):
                                        turn_sums(g - 1)
                        head_loop(pe, body, c, True)
                    turn_sums(CH * H0 - 1)
        msk_stack.close()
        features_0.close()

        def norm_buffers(ph):
            R = [sb(ph, f"R{q}", [P, D]) for q in (0, 1)]
            xn = [sb(ph, f"xn{q}", [P, D]) for q in (0, 1)]
            st = [sb(ph, f"st{q}", [P, 10]) for q in (0, 1)]
            xin = [sb(ph, f"xin{q}", [P, D]) for q in (0, 1)]
            xt = [sb(ph, f"xt{q}", [128, KT, P]) for q in (0, 1)]
            bias = sb(ph, "bias", [P, D])
            w_sb = sb(ph, "w_sb", [128, KT, D])
            return R, xn, st, xin, xt, bias, w_sb

        def norm_store(pool, i, q, n, dst, st, xn):
            ln_power(pool, n, q, st)
            pool.wait_ge(ln_done, n + 1)
            pool.dma_start(dst[2 * i + q], xn[q][:, :]).then_inc(xn_stored[q], 16)

        def normed(dve, n, i, q, R, st, xn, phase):
            ln_tile(dve, n, q, R, st, xn)
            wait(dve, xn_stored[q], 16 * (phase * PAIRS + i))
            wait(dve, turned, n + T - 1)
            ln_write(dve, n, q, R, st, xn[q][:, :])

        L1 = ExitStack()
        HR, HL = sb(L1, "HR", [P, T, D], F32R), sb(L1, "HL", [P, T, D], F32R)
        h_hi = sem("h_hi")
        with ExitStack() as ph:
            R, xn, st, xin, xt, bias, w_sb = norm_buffers(ph)
            c_in = sem("e0_in")
            with nc.Block() as block:
                @block.sync
                def _(sp):
                    sp.dma_start(bias[:, :], b0.partition_broadcast(P)).then_inc(c_in, 16)
                    sp.dma_start(w_sb[:, :, :], w1).then_inc(c_in, 16)

                    def body(i):
                        for q in (0, 1):
                            wait(sp, r_full, 2 * i + q - 1)
                            sp.dma_start(xin[q][:, :], x[2 * i + q]).then_inc(x_in[q], 16)
                    pair_loop(sp, body, first=True)

                @block.vector
                def _(dve):
                    dve.wait_ge(c_in, 32)

                    def body(i):
                        for q in (0, 1):
                            j = 2 * i + q
                            dve.tensor_tensor(R[q][:, :], HB[0:P, j, :], bias[:, :], ALU.add).then_inc(r_half, 1)
                            dve.wait_ge(r_half, j + 1)
                            dve.wait_ge(x_in[q], 16 * (PAIRS + i + 1))
                            dve.scalar_tensor_tensor(out=R[q][:, :], in0=R[q][:, :], scalar=0.0, in1=xin[q][:, :],
                                                     op0=ALU.max, op1=ALU.add).then_inc(r_full, 1)
                            normed(dve, j, i, q, R, st, xn, 0)
                            if not (isinstance(i, int) and j == 0):
                                h_out(j - 1)

                    def h_out(j):
                        dve.wait_ge(h_hi, j + 1)
                        dve.tensor_tensor(HL[:, j, :], pj[0:P, :], HR[:, j, :].bitcast(FP32), ALU.subtract)\
                           .then_inc(proj_out, 1)
                    pair_loop(dve, body, first=True)
                    h_out(T - 1)

                @block.gpsimd
                def _(pool):
                    def body(i):
                        for q in (0, 1):
                            norm_store(pool, i, q, 2 * i + q, xs[0], st, xn)
                    pair_loop(pool, body)
                    for q in (0, 1):
                        pool.wait_ge(xn_stored[q], 16 * PAIRS)

                @block.tensor
                def _(pe):
                    pe.wait_ge(c_in, 32)

                    def body(i):
                        for q in (0, 1):
                            j = 2 * i + q
                            pe.wait_ge(ln_done, j + 1)
                            turn_tile(pe, T + j, xn[q])
                            project(pe, T + j, xt[q], w_sb, None, None, 0)
                    pair_loop(pe, body)

                @block.scalar
                def _(act):
                    def body(i):
                        for q in (0, 1):
                            j = 2 * i + q
                            keep_turned(act, T + j, xt[q])
                            act.wait_ge(proj_mm, T + j + 1)
                            act.activation(HR[:, j, :], pj[0:P, :], ACT.Copy).then_inc(h_hi, 1)
                    pair_loop(act, body)

        with ExitStack() as ph:
            R, xn, st, xin, xt, bias, w_sb = norm_buffers(ph)
            at = [sb(ph, f"at{q}", [P, T, P]) for q in (0, 1)]
            hi = [sb(ph, f"hi{half}", [P, HT, P], F32R) for half in (0, 1)]
            lo = [sb(ph, f"lo{half}", [P, HT, P], F32R) for half in (0, 1)]
            vb = sb(ph, "vb", [P, D])
            srow = [sb(ph, f"srow{q}", [1, P]) for q in (0, 1)]
            c_in, at_in, half_done = sem("l1_in"), sems("at_in"), sem("half_done")
            hi_ready, lo_ready = sem("hi_ready"), sem("lo_ready")

            def half_of(q, half):
                return at[q][:, half * HT:(half + 1) * HT, :]

            with nc.Block() as block:
                @block.sync
                def _(sp):
                    sp.dma_start(bias[:, :], b1.partition_broadcast(P)).then_inc(c_in, 16)
                    sp.dma_start(w_sb[:, :, :], fc_w).then_inc(c_in, 16)
                    sp.dma_start(vb[:, :], fc_b.partition_broadcast(P)).then_inc(c_in, 16)

                    def body(i):
                        for q in (0, 1):
                            j = 2 * i + q
                            wait(sp, half_done, 2 * (j - 1))
                            sp.dma_start(at[q][:, :, :], adj_tiles[j]).then_inc(at_in[q], 16)
                            wait(sp, r_full, T + j - 1)
                            sp.dma_start(xin[q][:, :], xs[0][j]).then_inc(x_in[q], 16)
                    pair_loop(sp, body, first=True)

                @block.tensor
                def _(pe):
                    pe.wait_ge(c_in, 48)

                    def tail(j, q, part):
                        n = 2 * T + j
                        if part == 0:
                            pe.wait_ge(ln_done, T + j + 1)
                            turn_tile(pe, n, xn[q])
                        else:
                            scores(n, j, q)

                    def scores(n, j, q):
                        pe.wait_ge(turned_out, n + 1)
                        wait(pe, score_out, 2 * (T + j))
                        for k in range(KT):
                            pe.matmul(sc[0:P, 0:1], xt[q][:, k, :], u2s[:, k, :], start=(k == 0), stop=(k == KT - 1))
                        for k in range(KT):
                            t = pe.matmul(sc[0:1, 16:16 + P], u2n[:, k, :], xt[q][:, k, :],
                                          start=(k == 0), stop=(k == KT - 1))
                        t.then_inc(score_mm, 1)
                        project(pe, n, xt[q], w_sb, None, None, 0)

                    def body(i):
                        for q in (0, 1):
                            j = 2 * i + q
                            wait(pe, r_half, T + j - 1)
                            for m in range(T):
                                half, c = divmod(m, HT)
                                if c == 0:
                                    pe.wait_ge(hi_ready, 2 * j + half + 1)
                                pe.matmul(acc[q][0:P, :], hi[half][:, c, :], HR[:, m, :], start=(m == 0), stop=False)
                                pe.matmul(acc[q][0:P, :], hi[half][:, c, :], HL[:, m, :], start=False, stop=False)
                                if c == 0:
                                    pe.wait_ge(lo_ready, 2 * j + half + 1)
                                mm = pe.matmul(acc[q][0:P, :], lo[half][:, c, :], HR[:, m, :],
                                               start=False, stop=(m == T - 1))
                                if c == HT - 1:
                                    mm.then_inc(half_done, 1)
                                if not (isinstance(i, int) and j == 0) and m in (9, 17):
                                    tail(j - 1, 1 - q, int(m == 17))
                    pair_loop(pe, body, first=True)
                    tail(T - 1, 1, 0)
                    tail(T - 1, 1, 1)

                @block.vector
                def _(dve):
                    dve.wait_ge(c_in, 48)

                    def v_out(j):
                        dve.wait_ge(proj_mm, 2 * T + j + 1)
                        dve.tensor_tensor(HB[0:P, j, :], pj[0:P, :], vb[:, :], ALU.add).then_inc(proj_out, 1)

                    def rest(j, q, half):
                        dve.wait_ge(hi_ready, 2 * j + half + 1)
                        wait(dve, half_done, 2 * j + half - 1)
                        dve.tensor_tensor(lo[half][:, :, :], half_of(q, half), hi[half][:, :, :].bitcast(FP32),
                                          ALU.subtract).then_inc(lo_ready, 1)

                    rest(0, 0, 0)
                    rest(0, 0, 1)
                    rest(1, 1, 0)

                    def body(i):
                        for q in (0, 1):
                            j = 2 * i + q
                            n = T + j
                            dve.wait_ge(half_done, 2 * (j + 1))
                            dve.tensor_tensor(R[q][:, :], acc[q][0:P, :], bias[:, :], ALU.add).then_inc(r_half, 1)
                            dve.wait_ge(r_half, n + 1)
                            dve.wait_ge(x_in[q], 16 * (2 * PAIRS + i + 1))
                            dve.tensor_tensor(R[q][:, :], R[q][:, :], xin[q][:, :], ALU.add).then_inc(r_full, 1)
                            ln_tile(dve, n, q, R, st, xn)
                            wait(dve, xn_stored[q], 16 * (PAIRS + i))
                            wait(dve, turned, n + T - 1)
                            ln_write(dve, n, q, R, st, xn[q][:, :])
                            if not (isinstance(i, int) and j + 1 >= T):
                                rest(j + 1, 1 - q, 1)
                            if not (isinstance(i, int) and j + 2 >= T):
                                rest(j + 2, q, 0)
                            v_out(j)
                    pair_loop(dve, body, last=True)

                @block.gpsimd
                def _(pool):
                    def body(i):
                        for q in (0, 1):
                            j = 2 * i + q
                            norm_store(pool, i, q, T + j, xs[1], st, xn)
                            pool.wait_ge(score_out, 2 * (T + j) + 2)
                            pool.dma_start(rows2[:, bass.ds(j * P, P)], srow[q][:, :]).then_inc(row_stored[q], 16)
                    pair_loop(pool, body)
                    for q in (0, 1):
                        pool.wait_ge(xn_stored[q], 16 * 2 * PAIRS)
                        pool.wait_ge(row_stored[q], 16 * 2 * PAIRS)

                @block.scalar
                def _(act):
                    def rounded(j, i, q, half):
                        act.wait_ge(at_in[q], 16 * (i + 1))
                        wait(act, half_done, 2 * j + half - 1)
                        act.activation(hi[half][:, :, :], half_of(q, half), ACT.Copy).then_inc(hi_ready, 1)

                    rounded(0, 0, 0, 0)
                    rounded(0, 0, 0, 1)
                    rounded(1, 0, 1, 0)

                    def body(i):
                        for q in (0, 1):
                            j = 2 * i + q
                            if not (isinstance(i, int) and j + 1 >= T):
                                rounded(j + 1, i + q, 1 - q, 1)
                            keep_turned(act, 2 * T + j, xt[q])
                            if not (isinstance(i, int) and j + 2 >= T):
                                rounded(j + 2, i + 1, q, 0)
                            act.wait_ge(score_mm, T + j + 1)
                            act.activation(s1[0:P, bass.ds(j, 1)], sc[0:P, 0:1], ACT.Identity, bias=ab2[0:P, :])\
                               .then_inc(score_out, 1)
                            act.wait_ge(row_stored[q], 16 * (PAIRS + i))
                            act.activation(srow[q][:, :], sc[0:1, 16:16 + P], ACT.Copy).then_inc(score_out, 1)
                    pair_loop(act, body, last=True)
        L1.close()

        with ExitStack() as ph:
            R, xn, st, xin, xt, _, w_sb = norm_buffers(ph)
            rows = [sb(ph, f"rows{q}", [P, NP]) for q in (0, 1)]
            pr = [sb(ph, f"pr{q}", [P, NP]) for q in (0, 1)]
            pt = [sb(ph, f"pt{q}", [P, T, P]) for q in (0, 1)]
            stage, xw_stored = [sb(ph, f"stage{q}", [P, D]) for q in (0, 1)], sems("xw_stored")
            sB2 = sb(ph, "sB2", [P, NP])
            stat = [sb(ph, f"stat{q}", [P, 4]) for q in (0, 1)]
            sums = sb(ph, "sums", [P, T])
            srow = [sb(ph, f"srow{q}", [H3, P]) for q in (0, 1)]
            c_in, rows_in = sem("l2_in"), sems("l2_rows_in")
            neg_ready, z_ready, leaky_ready, max_ready, nmax_ready, p2_ready, rsum_ready = (
                sem(f"l2_{k}") for k in ("neg", "z", "leaky", "max", "nmax", "p", "rsum"))
            t_grp, t_out, m_grp = sem("l2_t_grp"), sem("l2_t_out"), sem("l2_m_grp")
            with nc.Block() as block:
                @block.sync
                def _(sp):
                    sp.dma_start(sB2[:, :], rows2[0, :].partition_broadcast(P)).then_inc(c_in, 16)
                    sp.dma_start(w_sb[:, 0, :], w3).then_inc(c_in, 16)

                    def body(i):
                        for q in (0, 1):
                            j = 2 * i + q
                            wait(sp, max_ready, j - 1)
                            sp.dma_start(rows[q][:, :], adj_rows[j]).then_inc(rows_in[q], 16)
                            wait(sp, r_full, 2 * T + j - 1)
                            sp.dma_start(xin[q][:, :], xs[1][j]).then_inc(x_in[q], 16)
                    pair_loop(sp, body, first=True)

                @block.scalar
                def _(act):
                    act.wait_ge(c_in, 32)

                    def z(j, q):
                        wait(act, t_grp, NG * (j - 1))
                        act.activation(pr[q][:, :], sB2[:, :], ACT.Identity, bias=s1[0:P, bass.ds(j, 1)])\
                           .then_inc(z_ready, 1)

                    def expo(j, q):
                        act.wait_ge(nmax_ready, j + 1)
                        act.activation(pr[q][:, :], pr[q][:, :], ACT.Exp, bias=stat[q][:, 1:2],
                                       accum_out=sums[:, bass.ds(j, 1)]).then_inc(p2_ready, 1)

                    def tail(j, q):
                        keep_turned(act, 3 * T + j, xt[q])
                        act.wait_ge(score_mm, 2 * T + j + 1)
                        act.activation(f1[0:P, j, :], sc[0:P, 0:H3], ACT.Copy).then_inc(score_out, 1)
                        act.wait_ge(row_stored[q], 16 * (2 * PAIRS + (j - q) // 2) if isinstance(j, int)
                                    else 16 * (2 * PAIRS) + (j - q) * 8)
                        act.activation(srow[q][:, :], sc[0:H3, 16:16 + P], ACT.Copy).then_inc(score_out, 1)

                    def body(i):
                        for q in (0, 1):
                            j = 2 * i + q
                            ahead = not (isinstance(i, int) and j + 2 >= T)
                            if ahead:
                                z(j + 2, q)
                            if not (isinstance(i, int) and j == 0):
                                tail(j - 1, 1 - q)
                            if ahead:
                                expo(j + 2, q)
                    for j in (0, 1):
                        z(j, j)
                        expo(j, j)
                    pair_loop(act, body, first=True, last=True)
                    tail(T - 1, 1)

                @block.vector
                def _(dve):
                    def missing(j, i, q):
                        dve.wait_ge(rows_in[q], 16 * (i + 1))
                        dve.tensor_scalar(rows[q][:, 0:N], rows[q][:, 0:N], 0.0, NEG, ALU.is_le, ALU.mult)\
                           .then_inc(neg_ready, 1)
                        dve.memset(rows[q][:, N:NP], LOW).then_inc(neg_ready, 1)

                    def leaky(j, q):
                        dve.wait_ge(z_ready, j + 1)
                        dve.scalar_tensor_tensor(out=pr[q][:, :], in0=pr[q][:, :], scalar=0.2, in1=pr[q][:, :],
                                                 op0=ALU.mult, op1=ALU.max).then_inc(leaky_ready, 1)

                    def masked_max(j, q):
                        scored, masked = count(dve, j + 1), count(dve, 2 * j + 2)
                        carry(dve, set_const, 1)
                        dve.wait_ge(leaky_ready, scored)
                        dve.wait_ge(neg_ready, masked)
                        dve.tensor_tensor_reduce(pr[q][:, :], pr[q][:, :], rows[q][:, :], 1.0, LOW, ALU.add, ALU.max,
                                                 stat[q][:, 0:1]).then_inc(max_ready, 1)
                        dve.wait_ge(max_ready, j + 1)
                        dve.tensor_scalar(stat[q][:, 1:2], stat[q][:, 0:1], -1.0, None, ALU.mult)\
                           .then_inc(nmax_ready, 1)

                    def keep(j, g):
                        u = NG * j + g
                        a, b = GROUPS[g]
                        dve.wait_ge(t_grp, u + 1)
                        wait(dve, m_grp, u - 2 * NG + 1)
                        dve.tensor_copy(pt[par(j)][:, a:b, :],
                                        turn[g % 3][0:P, 0:(b - a) * P].rearrange("p (t n) -> p t n", n=P))\
                           .then_inc(t_out, 1)

                    parity = {}

                    def par(j):
                        return j % 2 if isinstance(j, int) else parity["q"]

                    def result(j, q):
                        n = 2 * T + j
                        dve.wait_ge(m_grp, NG * (j + 1))
                        dve.wait_ge(p2_ready, j + 1)
                        dve.reciprocal(stat[q][:, 3:4], sums[:, bass.ds(j, 1)]).then_inc(rsum_ready, 1)
                        dve.wait_ge(rsum_ready, j + 1)
                        dve.wait_ge(x_in[q], (16 * 3 * PAIRS + 16 * (j - q) // 2 + 16) if isinstance(j, int)
                                    else (j - q) * 8 + 16 * 3 * PAIRS + 16)
                        dve.scalar_tensor_tensor(out=R[q][:, :], in0=acc[q][0:P, :], scalar=stat[q][:, 3:4],
                                                 in1=xin[q][:, :], op0=ALU.mult, op1=ALU.add).then_inc(r_full, 1)
                        ln_tile(dve, n, q, R, st, xn)
                        wait(dve, xn_stored[q], (16 * 2 * PAIRS + 8 * (j - q)) if isinstance(j, int)
                             else (j - q) * 8 + 16 * 2 * PAIRS)
                        wait(dve, turned, n + T - 1)
                        ln_write(dve, n, q, R, st, xn[q][:, :])

                    def xw_out(j, q):
                        dve.wait_ge(proj_mm, 3 * T + j + 1)
                        wait(dve, xw_stored[q], 8 * (j - q))
                        dve.tensor_copy(stage[q][:, :], pj[0:P, :]).then_inc(proj_out, 1)

                    for j in (0, 1):
                        missing(j, 0, j)
                        leaky(j, j)
                        masked_max(j, j)
                    for g in range(NG):
                        keep(0, g)

                    def body(i):
                        for q in (0, 1):
                            j = 2 * i + q
                            head = isinstance(i, int) and j == 0
                            ahead = not (isinstance(i, int) and j + 2 >= T)
                            for g in range(NG):
                                if not (isinstance(i, int) and j + 1 >= T):
                                    parity["q"] = 1 - q
                                    keep(j + 1, g)
                                if g == 0 and not head:
                                    result(j - 1, 1 - q)
                                if g == 1 and ahead:
                                    missing(j + 2, i + 1, q)
                                if g == 2 and ahead:
                                    leaky(j + 2, q)
                                if g == 4 and ahead:
                                    masked_max(j + 2, q)
                                if g == 5 and not head:
                                    xw_out(j - 1, 1 - q)
                    pair_loop(dve, body, first=2, last=True)
                    result(T - 1, 1)
                    xw_out(T - 1, 1)

                @block.tensor
                def _(pe):
                    pe.wait_ge(c_in, 32)

                    def turn_group(j, q, g):
                        u = NG * j + g
                        a, b = GROUPS[g]
                        if g == 0:
                            pe.wait_ge(p2_ready, j + 1)
                        wait(pe, t_out, u - 2)
                        for m in range(a, b):
                            t = pe.transpose(turn[g % 3][0:P, (m - a) * P:(m - a + 1) * P],
                                             pr[q][:, m * P:(m + 1) * P], idt[0:P, 0:P])
                        t.then_inc(t_grp, 1)

                    def mul_group(j, q, g):
                        a, b = GROUPS[g]
                        pe.wait_ge(t_out, NG * j + g + 1)
                        if g == 0:
                            wait(pe, r_full, 2 * T + j - 1)
                        for m in range(a, b):
                            t = pe.matmul(acc[q][0:P, :], pt[q][:, m, :], HB[0:P, m, :],
                                          start=(m == 0), stop=(m == T - 1))
                        t.then_inc(m_grp, 1)

                    def tail(j, q, part):
                        n = 3 * T + j
                        if part == 0:
                            pe.wait_ge(ln_done, 2 * T + j + 1)
                            turn_tile(pe, n, xn[q])
                            return
                        pe.wait_ge(turned_out, n + 1)
                        wait(pe, score_out, 2 * (2 * T + j))
                        for k in range(KT):
                            pe.matmul(sc[0:P, 0:H3], xt[q][:, k, :], u3s[:, k, :], start=(k == 0), stop=(k == KT - 1))
                        for k in range(KT):
                            t = pe.matmul(sc[0:H3, 16:16 + P], u3n[:, k, :], xt[q][:, k, :],
                                          start=(k == 0), stop=(k == KT - 1))
                        t.then_inc(score_mm, 1)
                        project(pe, n, xt[q], w_sb[:, 0, :].rearrange("p (h e) -> p h e", e=D3), None, None, 0,
                                blocked=True)

                    for g in range(NG):
                        turn_group(0, 0, g)

                    def body(i):
                        for q in (0, 1):
                            j = 2 * i + q
                            head = isinstance(i, int) and j == 0
                            for g in range(NG):
                                if not (isinstance(i, int) and j + 1 >= T):
                                    turn_group(j + 1, 1 - q, g)
                                mul_group(j, q, g)
                                if g == 2 and not head:
                                    tail(j - 1, 1 - q, 0)
                                if g == 4 and not head:
                                    tail(j - 1, 1 - q, 1)
                    pair_loop(pe, body, first=True, last=True)
                    tail(T - 1, 1, 0)
                    tail(T - 1, 1, 1)

                @block.gpsimd
                def _(pool):
                    def body(i):
                        for q in (0, 1):
                            j = 2 * i + q
                            norm_store(pool, i, q, 2 * T + j, xs[2], st, xn)
                            pool.wait_ge(score_out, 2 * (2 * T + j) + 2)
                            pool.dma_start(rows3[:, bass.ds(j * P, P)], srow[q][:, :]).then_inc(row_stored[q], 16)
                            made = count(pool, 3 * T + j + 1)
                            carry(pool, set_const, 1)
                            pool.wait_ge(proj_out, made)
                            pool.dma_start(xw_dram[j], stage[q][:, :]).then_inc(xw_stored[q], 16)
                    pair_loop(pool, body)
                    for q in (0, 1):
                        pool.wait_ge(xn_stored[q], 16 * 3 * PAIRS)
                        pool.wait_ge(row_stored[q], 16 * 3 * PAIRS)
                        pool.wait_ge(xw_stored[q], 16 * PAIRS)
        L0.close()

        HA = sb(top, "HA", [P, T, D])
        a_bn = [sb(top, f"a_bn{k}", [P, D]) for k in range(2)]
        shift = sb(top, "shift", [P, D])
        lin, quad = sb(top, "lin", [P, D]), sb(top, "quad", [P, D])
        shift_mm, shift_ready = sem("shift_mm"), sem("shift_ready")
        st_y, st_lin, st_sq, st_quad = (sem(f"stats_{k}") for k in ("y", "lin", "sq", "quad"))
        bn_zero, bn_sum, bn_step, bn_pow, bn_row = (sem(f"bn_{k}") for k in ("zero", "sum", "step", "pow", "row"))
        xc_ready, row_out, gb_in = sem("xc_ready"), sem("bn_row_out"), sem("gb_in")
        gb = sb(top, "gb", [128, 2, 3, KT])
        bnf = sb(top, "bnf", [128, 4, KT])

        def stats_tile(pool, n, y, src, count):
            pool.wait_ge(xc_ready, n + 1)
            pool.tensor_tensor(y[0][0:count, :], src, shift[0:count, :], ALU.subtract).then_inc(st_y, 1)
            pool.wait_ge(st_y, n + 1)
            wait(pool, st_lin, n)
            pool.tensor_tensor(lin[0:count, :], lin[0:count, :], y[0][0:count, :], ALU.add).then_inc(st_lin, 1)
            pool.tensor_tensor(y[1][0:count, :], y[0][0:count, :], y[0][0:count, :], ALU.mult).then_inc(st_sq, 1)
            pool.wait_ge(st_sq, n + 1)
            wait(pool, st_quad, n)
            pool.tensor_tensor(quad[0:count, :], quad[0:count, :], y[1][0:count, :], ALU.add).then_inc(st_quad, 1)

        def shift_matmul(pe, k, src):
            pe.wait_ge(xc_ready, k * T + 1)
            pe.matmul(bank[7][0:P, :], ones[0:P, 0:P], src, start=True, stop=True).then_inc(shift_mm, 1)

        def shift_out(dve, k):
            dve.wait_ge(shift_mm, k + 1)
            dve.tensor_scalar(shift[:, :], bank[7][0:P, :], 1.0 / P, None, ALU.mult).then_inc(shift_ready, 1)

        def sums_clear(pool, k):
            pool.memset(lin[:, :], 0.0).then_inc(bn_zero, 1)
            pool.memset(quad[:, :], 0.0).then_inc(bn_zero, 1)
            pool.wait_ge(bn_zero, 2 * k + 2)

        def bn_total(pe, k):
            pe.wait_ge(st_quad, (k + 1) * T)
            pe.wait_ge(st_lin, (k + 1) * T)
            for part, src in enumerate((lin, quad, shift)):
                for c in range(KT):
                    t = pe.matmul(bank[6][:, part * KT + c:part * KT + c + 1], src[:, c * 128:(c + 1) * 128],
                                  ones[0:P, 0:1], start=True, stop=True)
            t.then_inc(bn_sum, 1)
            for part in range(2):
                pe.wait_ge(bn_step, 8 * k + 6 + 2 * part)
                for c in range(KT):
                    t = pe.matmul(bank[7 - part][0:P, c * 128:(c + 1) * 128],
                                  bnf[:, part, c:c + 1].broadcast_to([128, P]), idt[:, :], start=True, stop=True)
                t.then_inc(bn_row, 1)

        def bn_finish(dve, k):
            f = [8 * k]
            scale, offset, mean, var = (bnf[:, c, :] for c in range(4))
            total = [bank[6][:, c * KT:(c + 1) * KT] for c in range(3)]

            def step(ins):
                ins.then_inc(bn_step, 1)
                f[0] += 1
                dve.wait_ge(bn_step, f[0])
            dve.wait_ge(bn_sum, k + 1)
            step(dve.tensor_scalar(mean, total[0], 1.0 / N, None, ALU.mult))
            step(dve.tensor_tensor(var, mean, mean, ALU.mult))
            step(dve.scalar_tensor_tensor(out=var, in0=total[1], scalar=1.0 / N, in1=var,
                                          op0=ALU.mult, op1=ALU.subtract))
            step(dve.tensor_scalar(var, var, BN_EPS, None, ALU.add))
            step(dve.scalar_tensor_tensor(out=mean, in0=total[2], scalar=1.0 / P, in1=mean,
                                          op0=ALU.mult, op1=ALU.add))
            dve.wait_ge(bn_pow, k + 1)
            dve.wait_ge(gb_in, 32)
            step(dve.tensor_tensor(scale, gb[:, 0, k, :], var, ALU.mult))
            step(dve.tensor_tensor(mean, mean, scale, ALU.mult))
            step(dve.tensor_tensor(offset, gb[:, 1, k, :], mean, ALU.subtract))
            for part in range(2):
                dve.wait_ge(bn_row, 2 * k + part + 1)
                dve.tensor_copy(a_bn[part][:, :], bank[7 - part][0:P, :]).then_inc(row_out, 1)
            dve.wait_ge(row_out, 2 * k + 2)

        def bn_power(pool, k):
            pool.wait_ge(bn_step, 8 * k + 4)
            pool.tensor_tensor(bnf[:, 3, :], bnf[:, 3, :], half[:, 0:1].broadcast_to([128, KT]), ALU.pow)\
                .then_inc(bn_pow, 1)

        weights = scratch("weights", [H3 * T, P, T, P])
        edge_ready = sem("edge_ready")
        ri = sb(top, "ri", [P, T, H3])
        has_edge = sb(top, "has_edge", [P, T])
        with ExitStack() as ph:
            rows = [sb(ph, f"rows{q}", [P, NP]) for q in (0, 1)]
            low = [sb(ph, f"low{q}", [P, NP // 4]) for q in (0, 1)]
            fB = sb(ph, "fB", [P, H3, NP])
            v = [sb(ph, f"v{h}", [P, NP]) for h in range(H3 + 1)]
            pt = [sb(ph, f"pt{q}", [P, T, P]) for q in (0, 1)]
            mx = [sb(ph, f"mx{q}", [P, H3]) for q in (0, 1)]
            nm, rs, rc = (sb(ph, n_, [P, T, H3]) for n_ in ("nm", "rs", "rc"))
            xc = [sb(ph, f"xc{q}", [P, D]) for q in (0, 1)]
            y = a_bn
            ha_in, first_adj = sem("ha_in"), sem("first_adj")
            fb_in, rows_in = [sem(f"att_in{h}") for h in range(H3)], sems("att_rows_in")
            low_ready, adj_ready, sig_ready, mx_ready, nm_ready, p_ready = (
                sem(f"att_{k}") for k in ("low", "adj", "sig", "mx", "nm", "p"))
            t_grp, t_out, m_grp = sem("att_t_grp"), sem("att_t_out"), sem("att_m_grp")
            rc_ready, ri_ready = sem("att_rc"), sem("att_ri")
            stored = sems("att_stored")
            C4 = NP // 4

            def weights_of(h, q):
                return v[h + q if h == H3 - 1 else h]

            weights_stored = sems("weights_stored")
            with nc.Block() as block:
                @block.sync
                def _(sp):
                    sp.dma_start(gb[:, 0, :, :], g_bn).then_inc(gb_in, 16)
                    sp.dma_start(gb[:, 1, :, :], b_bn).then_inc(gb_in, 16)

                    def load(i, q):
                        wait(sp, mx_ready, H3 * (2 * i + q - 1))
                        sp.dma_start(rows[q][:, :], adj_rows[2 * i + q]).then_inc(rows_in[q], 16)

                    def store(j, q):
                        sp.wait_ge(xc_ready, j + 1)
                        sp.dma_start(xc_dram[j], xc[q][:, :]).then_inc(stored[q], 16)

                    def body(i):
                        for q in (0, 1):
                            if not (isinstance(i, int) and i + 1 >= PAIRS):
                                load(i + 1, q)
                            if not (isinstance(i, int) and 2 * i + q == 0):
                                store(2 * i + q - 1, 1 - q)
                            for h in range(H3):
                                s = H3 * (2 * i + q) + h
                                sp.wait_ge(t_out, NG * (s + 1))
                                sp.dma_start(weights[s], pt[h % 2][:, :, :]).then_inc(weights_stored[h % 2], 16)
                    load(0, 0)
                    for h in range(H3):
                        sp.dma_start(fB[:, h, :], rows3[h, :].partition_broadcast(P)).then_inc(fb_in[h], 16)
                    load(0, 1)
                    sp.dma_start(HA[:, :, :], xw_dram.rearrange("t p d -> p t d")).then_inc(ha_in, 16)
                    pair_loop(sp, body, first=True, last=True)
                    store(T - 1, 1)
                    for q in (0, 1):
                        sp.wait_ge(stored[q], 16 * PAIRS)
                        sp.wait_ge(weights_stored[q], 16 * H3 * PAIRS)

                @block.gpsimd
                def _(pool):
                    def absent(i, q):
                        j = 2 * i + q
                        loaded = count(pool, 16 * (i + 1))
                        carry(pool, set_const, 1)
                        pool.wait_ge(rows_in[q], loaded)
                        for c in range(4):
                            part = rows[q][:, c * C4:(c + 1) * C4]
                            pool.tensor_scalar(low[c % 2][:, :], part, 0.0, LOW, ALU.is_equal, ALU.mult)\
                                .then_inc(low_ready, 1)
                            pool.wait_ge(low_ready, 4 * j + c - 3)
                            pool.tensor_tensor(part, part, low[c % 2][:, :], ALU.add).then_inc(adj_ready, 1)

                    def tile_stats(j, q, count=P):
                        if isinstance(j, int) and j == 0:
                            pool.wait_ge(shift_ready, 1)
                        stats_tile(pool, j, y, xc[q][0:count, :], count)

                    def body(i):
                        for q in (0, 1):
                            j = 2 * i + q
                            if not (isinstance(i, int) and j == 0):
                                tile_stats(j - 1, 1 - q)
                            if not (isinstance(i, int) and i + 1 >= PAIRS):
                                absent(i + 1, q)
                    absent(0, 1)
                    sums_clear(pool, 0)
                    pair_loop(pool, body, first=True, last=True)
                    tile_stats(T - 1, 1, TAIL)
                    bn_power(pool, 0)

                @block.scalar
                def _(act):
                    def body(i):
                        for q in (0, 1):
                            j = 2 * i + q
                            for h in range(H3):
                                before = j - 2 if h == H3 - 1 else j - 1
                                wait(act, t_grp, NG * (H3 * before + h + 1))
                                if isinstance(i, int) and j == 0:
                                    act.wait_ge(fb_in[h], 16)
                                if isinstance(i, int) and j == 1 and h == H3 - 1:
                                    act.wait_ge(first_adj, 2)
                                act.activation(weights_of(h, q)[:, :], fB[:, h, :], ACT.Sigmoid, bias=f1[0:P, j, h:h + 1])\
                                   .then_inc(sig_ready, 1)
                            for h in range(H3):
                                act.wait_ge(nm_ready, H3 * j + h + 1)
                                act.activation(weights_of(h, q)[:, :], weights_of(h, q)[:, :], ACT.Exp, bias=nm[:, j, h:h + 1],
                                               accum_out=rs[:, j, h:h + 1]).then_inc(p_ready, 1)
                    pair_loop(act, body, first=True)

                @block.vector
                def _(dve):
                    def weigh(j, q, h):
                        s = H3 * j + h
                        masked, scored = count(dve, 4 * j), count(dve, s + 1)
                        carry(dve, set_const, 1)
                        if h == 0 and isinstance(j, int) and j == 0:
                            dve.wait_ge(first_adj, 2)
                        elif h == 0:
                            dve.wait_ge(adj_ready, masked)
                        dve.wait_ge(sig_ready, scored)
                        v_h = weights_of(h, q)
                        dve.tensor_tensor_reduce(v_h[:, :], v_h[:, :], rows[q][:, :], 1.0, LOW, ALU.mult, ALU.max,
                                                 mx[q][:, h:h + 1]).then_inc(mx_ready, 1)
                        dve.wait_ge(mx_ready, s + 1)
                        dve.tensor_scalar(nm[:, j, h:h + 1], mx[q][:, h:h + 1], -1.0, None, ALU.mult)\
                           .then_inc(nm_ready, 1)

                    def keep(s, g, k):
                        u = NG * s + g
                        a, b = GROUPS[g]
                        dve.wait_ge(t_grp, u + 1)
                        wait(dve, m_grp, u - 2 * NG + 1)
                        if g == 0:
                            stores = s // 2 if isinstance(s, int) else 8 * s - 8 * k
                            wait(dve, weights_stored[k], 16 * stores if isinstance(s, int) else stores)
                        dve.tensor_copy(pt[k][:, a:b, :],
                                        turn[g % 3][0:P, 0:(b - a) * P].rearrange("p (t n) -> p t n", n=P))\
                           .then_inc(t_out, 1)

                    def result(j, q):
                        dve.wait_ge(p_ready, H3 * (j + 1))
                        dve.reciprocal(rc[:, j, :], rs[:, j, :]).then_inc(rc_ready, 1)
                        dve.wait_ge(rc_ready, j + 1)
                        dve.scalar_tensor_tensor(out=ri[:, j, :], in0=nm[:, j, :], scalar=1e20, in1=rc[:, j, :],
                                                 op0=ALU.is_lt, op1=ALU.mult).then_inc(ri_ready, 1)
                        dve.wait_ge(ri_ready, j + 1)
                        dve.wait_ge(m_grp, NG * H3 * (j + 1))
                        if isinstance(j, int):
                            wait(dve, stored[q], 16 * (j // 2))
                        else:
                            dve.wait_ge(stored[q], (j - q) * 8)
                        wait(dve, st_y, j - 1)
                        dve.tensor_tensor(xc[q][:, :].rearrange("p (h e) -> p h e", e=D3),
                                          acc[q][0:P, :].rearrange("p (h e) -> p h e", e=D3),
                                          ri[:, j, :].unsqueeze(2).broadcast_to([P, H3, D3]),
                                          ALU.mult).then_inc(xc_ready, 1)

                    dve.wait_ge(rows_in[0], 16)
                    dve.tensor_scalar(v[H3][:, :], rows[0][:, :], 0.0, LOW, ALU.is_equal, ALU.mult).then_inc(first_adj, 1)
                    dve.wait_ge(first_adj, 1)
                    dve.tensor_tensor(rows[0][:, :], rows[0][:, :], v[H3][:, :], ALU.add).then_inc(first_adj, 1)
                    for h in range(H3):
                        weigh(0, 0, h)
                    for g in range(NG):
                        keep(0, g, 0)

                    def body(i):
                        for q in (0, 1):
                            j = 2 * i + q
                            head = isinstance(i, int) and j == 0
                            final = isinstance(i, int) and j == T - 1
                            for h in range(H3):
                                if h == H3 - 1 and not final:
                                    weigh(j + 1, 1 - q, h)
                                for g in range(NG):
                                    if not (final and h == H3 - 1):
                                        keep(H3 * j + h + 1, g, (h + 1) % 2)
                                    if h == 0 and g == 1 and not head:
                                        result(j - 1, 1 - q)
                                    if isinstance(i, int) and j == 1 and h == 1 and g == 1:
                                        shift_out(dve, 0)
                                    if g == 2 and h < H3 - 1 and not final:
                                        weigh(j + 1, 1 - q, h)
                    pair_loop(dve, body, first=2, last=True)
                    result(T - 1, 1)
                    dve.tensor_scalar(has_edge[:, :], nm[:, :, 0], 1e20, None, ALU.is_lt).then_inc(edge_ready, 1)
                    dve.wait_ge(edge_ready, 1)
                    bn_finish(dve, 0)

                @block.tensor
                def _(pe):
                    def turn_group(s, q, h, g):
                        u = NG * s + g
                        a, b = GROUPS[g]
                        if g == 0:
                            pe.wait_ge(p_ready, s + 1)
                        wait(pe, t_out, u - 2)
                        for m in range(a, b):
                            t = pe.transpose(turn[g % 3][0:P, (m - a) * P:(m - a + 1) * P],
                                             weights_of(h, q)[:, m * P:(m + 1) * P], idt[0:P, 0:P])
                        t.then_inc(t_grp, 1)

                    def mul_group(j, q, h, g):
                        a, b = GROUPS[g]
                        pe.wait_ge(t_out, NG * (H3 * j + h) + g + 1)
                        if h == 0 and g == 0:
                            wait(pe, xc_ready, j - 1)
                        for m in range(a, b):
                            t = pe.matmul(acc[q][0:P, h * D3:(h + 1) * D3], pt[h % 2][:, m, :],
                                          HA[0:P, m, h * D3:(h + 1) * D3], start=(m == 0), stop=(m == T - 1))
                        t.then_inc(m_grp, 1)

                    for g in range(NG):
                        turn_group(0, 0, 0, g)
                    pe.wait_ge(ha_in, 16)

                    def body(i):
                        for q in (0, 1):
                            j = 2 * i + q
                            final = isinstance(i, int) and j == T - 1
                            for h in range(H3):
                                nxt = not (final and h == H3 - 1)
                                for g in range(NG):
                                    if nxt:
                                        turn_group(H3 * j + h + 1, q, (h + 1) % H3, g)
                                    mul_group(j, q, h, g)
                                if isinstance(i, int) and j == 1 and h == 0:
                                    shift_matmul(pe, 0, xc[0][:, :])
                    pair_loop(pe, body, first=True, last=True)
                    bn_total(pe, 0)


        def from_shift(dve, n, j, q, y, count=P):
            dve.wait_ge(xc_ready, n + 1)
            wait(dve, st_lin, n - 1)
            wait(dve, st_sq, n - 1)
            dve.tensor_tensor(y[q][0:count, :], HA[0:count, j, 0:D], shift[0:count, :], ALU.subtract).then_inc(st_y, 1)

        def square(act, n, q, y, ysq, count=P):
            act.wait_ge(st_y, n + 1)
            wait(act, st_quad, n - 1)
            act.activation(ysq[q][0:count, :], y[q][0:count, :], ACT.Square).then_inc(st_sq, 1)

        def add_sums(pool, n, q, y, ysq, count=P):
            pool.wait_ge(st_y, n + 1)
            wait(pool, st_lin, n)
            pool.tensor_tensor(lin[0:count, :], lin[0:count, :], y[q][0:count, :], ALU.add).then_inc(st_lin, 1)
            pool.wait_ge(st_sq, n + 1)
            wait(pool, st_quad, n)
            pool.tensor_tensor(quad[0:count, :], quad[0:count, :], ysq[q][0:count, :], ALU.add).then_inc(st_quad, 1)

        def sums_loop(pool, base, y, ysq):
            def body(i):
                for q in (0, 1):
                    j = 2 * i + q
                    add_sums(pool, base + j, q, y, ysq, TAIL if isinstance(i, int) and j == T - 1 else P)
            pair_loop(pool, body, last=True)

        def elu_parts(ph):
            return [[sb(ph, f"{n_}{q}", [P, D]) for q in (0, 1)] for n_ in ("z", "e", "u")]

        pj_of = (pj, bank[4])

        with ExitStack() as ph:
            z, e, u = elu_parts(ph)
            XB = sb(ph, "XB", [P, T, D])
            xb = [sb(ph, f"xb{q}", [P, D]) for q in (0, 1)]
            xt = [sb(ph, f"xt{q}", [128, KT, P]) for q in (0, 1)]
            y = [sb(ph, f"y{q}", [P, D]) for q in (0, 1)]
            ysq = [sb(ph, f"ysq{q}", [P, D]) for q in (0, 1)]
            w_sb, bias = sb(ph, "w_sb", [128, KT, D]), sb(ph, "bias", [P, D])
            c_in, m_in = sem("mlp1_in"), sems("mlp1_x_in")
            xa_ready, xb_ready, z_ready, e_ready, u_ready = (sem(f"mlp1_{k}") for k in ("xa", "xb", "z", "e", "u"))
            put_ready = sem("mlp1_put")
            tr, tr_out, mm_done = sem("mlp1_turned"), sem("mlp1_turned_out"), sem("mlp1_mm")
            with nc.Block() as block:
                @block.sync
                def _(sp):
                    first_tiles, other_tiles = xc_dram[0:4], xc_dram[4:T]
                    sp.dma_start(XB[:, 0:4, :], first_tiles.rearrange("t p d -> p t d")).then_inc(m_in[0], 16)
                    sp.dma_start(w_sb[:, :, :], enc_w).then_inc(c_in, 16)
                    sp.dma_start(bias[:, :], enc_b.partition_broadcast(P)).then_inc(c_in, 16)
                    sp.dma_start(XB[:, 4:T, :], other_tiles.rearrange("t p d -> p t d")).then_inc(m_in[1], 16)

                @block.vector
                def _(dve):
                    def norm(j):
                        dve.tensor_tensor(XB[:, j, :], XB[:, j, :], a_bn[0][:, :], ALU.mult).then_inc(xa_ready, 1)
                        dve.wait_ge(xa_ready, j + 1)
                        dve.tensor_tensor(XB[:, j, :], XB[:, j, :], a_bn[1][:, :], ALU.add).then_inc(xb_ready, 1)

                    def linear(j, q):
                        dve.wait_ge(mm_done, j + 1)
                        wait(dve, e_ready, j - 1)
                        dve.tensor_tensor(z[q][:, :], pj_of[q][0:P, :], bias[:, :], ALU.add).then_inc(z_ready, 1)

                    def add(j, q):
                        dve.wait_ge(e_ready, j + 1)
                        dve.scalar_tensor_tensor(out=u[q][:, :], in0=e[q][:, :], scalar=1.0, in1=XB[:, j, :],
                                                 op0=ALU.min, op1=ALU.add).then_inc(u_ready, 1)
                        dve.wait_ge(u_ready, j + 1)
                        dve.scalar_tensor_tensor(out=HA[0:P, j, 0:D], in0=z[q][:, :], scalar=0.0, in1=u[q][:, :],
                                                 op0=ALU.max, op1=ALU.add).then_inc(xc_ready, 1)

                    def body(i):
                        for q in (0, 1):
                            j = 2 * i + q
                            if isinstance(i, int) and j == 2:
                                dve.wait_ge(m_in[1], 16)
                            if not (isinstance(i, int) and j + 2 >= T):
                                norm(j + 2)
                            linear(j, q)
                            add(j, q)
                            if not (isinstance(i, int) and j == 0):
                                if isinstance(i, int) and j == 1:
                                    shift_out(dve, 1)
                                    dve.wait_ge(shift_ready, 2)
                                from_shift(dve, T + j - 1, j - 1, 1 - q, y)
                    dve.wait_ge(m_in[0], 16)
                    norm(0)
                    norm(1)
                    dve.wait_ge(c_in, 32)
                    pair_loop(dve, body, first=2, last=True)
                    from_shift(dve, 2 * T - 1, T - 1, 1, y, TAIL)
                    bn_finish(dve, 1)

                @block.tensor
                def _(pe):
                    def turn_x(j, q):
                        pe.wait_ge(put_ready, j + 1)
                        wait(pe, tr_out, j)
                        for k in range(KT):
                            t = pe.transpose(etp_view()[:, k, :], xb[q][:, k * 128:(k + 1) * 128], idt[0:P, 0:P])
                        t.then_inc(tr, 1)

                    def mul(j, q):
                        pe.wait_ge(tr_out, j + 1)
                        wait(pe, z_ready, j - 1)
                        for k in range(KT):
                            t = pe.matmul(pj_of[q][0:P, :], xt[q][:, k, :], w_sb[:, k, :], start=(k == 0),
                                          stop=(k == KT - 1))
                        t.then_inc(mm_done, 1)

                    def body(i):
                        for q in (0, 1):
                            j = 2 * i + q
                            if not (isinstance(i, int) and j + 1 >= T):
                                turn_x(j + 1, 1 - q)
                            mul(j, q)
                            if isinstance(i, int) and j == 1:
                                shift_matmul(pe, 1, HA[0:P, 0, 0:D])
                    turn_x(0, 0)
                    pe.wait_ge(c_in, 32)
                    pair_loop(pe, body, first=True, last=True)
                    bn_total(pe, 1)

                @block.scalar
                def _(act):
                    def put_x(j, q):
                        act.wait_ge(xb_ready, j + 1)
                        wait(act, tr, j - 1)
                        act.activation(xb[q][:, :], XB[:, j, :], ACT.Copy).then_inc(put_ready, 1)

                    def copy_x(j, q):
                        act.wait_ge(tr, j + 1)
                        wait(act, mm_done, j - 1)
                        act.activation(xt[q][:, :, :], etp_view(), ACT.Copy).then_inc(tr_out, 1)

                    def expo(j, q):
                        act.wait_ge(z_ready, j + 1)
                        wait(act, u_ready, j - 1)
                        act.activation(e[q][:, :], z[q][:, :], ACT.Exp).then_inc(e_ready, 1)

                    def body(i):
                        for q in (0, 1):
                            j = 2 * i + q
                            if not (isinstance(i, int) and j + 1 >= T):
                                copy_x(j + 1, 1 - q)
                            if not (isinstance(i, int) and j + 2 >= T):
                                put_x(j + 2, q)
                            if not (isinstance(i, int) and j < 2):
                                square(act, T + j - 2, q, y, ysq)
                            expo(j, q)
                    put_x(0, 0)
                    put_x(1, 1)
                    copy_x(0, 0)
                    pair_loop(act, body, first=True, last=True)
                    square(act, 2 * T - 2, 0, y, ysq)
                    square(act, 2 * T - 1, 1, y, ysq, TAIL)

                @block.gpsimd
                def _(pool):
                    sums_clear(pool, 1)
                    sums_loop(pool, T, y, ysq)
                    bn_power(pool, 1)

        dec = ExitStack()
        XA = sb(dec, "XA", [P, T, D])
        with ExitStack() as ph:
            RING = 2 * H3
            w = [sb(ph, f"w{k}", [P, T, P]) for k in range(RING)]
            w_in = [sem(f"w_in{k}") for k in range(RING)]
            slot_done, att_out = sem("slot_done"), sem("att_out")
            with nc.Block() as block:
                @block.sync
                def _(sp):
                    def body(i):
                        for k in range(RING):
                            wait(sp, slot_done, RING * (i - 1) + k + 1)
                            sp.dma_start(w[k][:, :, :], weights[RING * i + k]).then_inc(w_in[k], 16)
                    pair_loop(sp, body, first=True)

                @block.tensor
                def _(pe):
                    def body(i):
                        for q in (0, 1):
                            for h in range(H3):
                                k = H3 * q + h
                                pe.wait_ge(w_in[k], 16 * (i + 1))
                                if h == 0:
                                    wait(pe, att_out, 2 * i + q - 1)
                                for m in range(T):
                                    t = pe.matmul(acc[q][0:P, h * D3:(h + 1) * D3], w[k][:, m, :],
                                                  HA[0:P, m, h * D3:(h + 1) * D3], start=(m == 0), stop=(m == T - 1))
                                t.then_inc(slot_done, 1)
                    pair_loop(pe, body, first=True)

                @block.vector
                def _(dve):
                    def body(i):
                        for q in (0, 1):
                            j = 2 * i + q
                            dve.wait_ge(slot_done, H3 * (j + 1))
                            dve.tensor_tensor(XA[:, j, :].rearrange("p (h e) -> p h e", e=D3),
                                              acc[q][0:P, :].rearrange("p (h e) -> p h e", e=D3),
                                              ri[:, j, :].unsqueeze(2).broadcast_to([P, H3, D3]),
                                              ALU.mult).then_inc(att_out, 1)
                    pair_loop(dve, body)


        with ExitStack() as ph:
            z, e, u = elu_parts(ph)
            xb, e1, u1, yc = ([sb(ph, f"{n_}{q}", [P, D]) for q in (0, 1)] for n_ in ("xb", "e1", "u1", "yc"))
            xt = [sb(ph, f"xt{q}", [128, KT, P]) for q in (0, 1)]
            yt = [sb(ph, f"yt{q}", [128, KT, P]) for q in (0, 1)]
            y = [sb(ph, f"y{q}", [P, D]) for q in (0, 1)]
            ysq = [sb(ph, f"ysq{q}", [P, D]) for q in (0, 1)]
            w_sb, bias = sb(ph, "w_sb", [128, KT, D]), sb(ph, "bias", [P, D])
            wt_sb = sb(ph, "wt_sb", [128, H3, D3])
            c_in = sem("mlp2_in")
            xa_ready, xb_ready, z_ready, e_ready, u_ready = (sem(f"mlp2_{k}") for k in ("xa", "xb", "z", "e", "u"))
            e1_ready, u1_ready, yc_ready = (sem(f"mlp2_{k}") for k in ("e1", "u1", "yc"))
            tr, tr_out, mm_done = sem("mlp2_turned"), sem("mlp2_turned_out"), sem("mlp2_mm")
            tr1, tr1_out, mm1_done = sem("mlp2_turned1"), sem("mlp2_turned1_out"), sem("mlp2_mm1")
            tp1, pj1_of = bank[2], (bank[3], bank[0])

            def tp1_view():
                return tp1[:, 0:KT * P].rearrange("p (k n) -> p k n", k=KT)

            with nc.Block() as block:
                @block.sync
                def _(sp):
                    sp.dma_start(wt_sb[:, :, :], w3t.rearrange("p (h d) -> p h d", h=H3)).then_inc(c_in, 16)
                    sp.dma_start(w_sb[:, :, :], dec_w).then_inc(c_in, 16)
                    sp.dma_start(bias[:, :], dec_b.partition_broadcast(P)).then_inc(c_in, 16)

                @block.vector
                def _(dve):
                    def norm(j, q):
                        dve.tensor_tensor(XA[:, j, :], XA[:, j, :], a_bn[0][:, :], ALU.mult).then_inc(xa_ready, 1)
                        dve.wait_ge(xa_ready, j + 1)
                        wait(dve, tr, j - 1)
                        dve.scalar_tensor_tensor(out=xb[q][:, :], in0=a_bn[1][:, :], scalar=has_edge[:, bass.ds(j, 1)],
                                                 in1=XA[:, j, :], op0=ALU.mult, op1=ALU.add).then_inc(xb_ready, 1)

                    def first_elu(j, q):
                        dve.wait_ge(e1_ready, j + 1)
                        dve.tensor_scalar(u1[q][:, :], e1[q][:, :], 1.0, -1.0, ALU.min, ALU.add).then_inc(u1_ready, 1)
                        dve.wait_ge(u1_ready, j + 1)
                        wait(dve, tr1, j - 1)
                        dve.scalar_tensor_tensor(out=yc[q][:, :], in0=pj1_of[q][0:P, :], scalar=0.0, in1=u1[q][:, :],
                                                 op0=ALU.max, op1=ALU.add).then_inc(yc_ready, 1)

                    def linear(j, q):
                        dve.wait_ge(mm_done, j + 1)
                        wait(dve, e_ready, j - 1)
                        dve.tensor_tensor(z[q][:, :], pj_of[q][0:P, :], bias[:, :], ALU.add).then_inc(z_ready, 1)

                    def add(j, q):
                        dve.wait_ge(e_ready, j + 1)
                        dve.scalar_tensor_tensor(out=u[q][:, :], in0=e[q][:, :], scalar=1.0, in1=yc[q][:, :],
                                                 op0=ALU.min, op1=ALU.add).then_inc(u_ready, 1)
                        dve.wait_ge(u_ready, j + 1)
                        dve.scalar_tensor_tensor(out=HA[0:P, j, 0:D], in0=z[q][:, :], scalar=0.0, in1=u[q][:, :],
                                                 op0=ALU.max, op1=ALU.add).then_inc(xc_ready, 1)

                    def body(i):
                        for q in (0, 1):
                            j = 2 * i + q
                            first_elu(j, q)
                            if not (isinstance(i, int) and j + 2 >= T):
                                norm(j + 2, q)
                            if not (isinstance(i, int) and j == 0):
                                linear(j - 1, 1 - q)
                                add(j - 1, 1 - q)
                            if isinstance(i, int) and j == 2:
                                shift_out(dve, 2)
                                dve.wait_ge(shift_ready, 3)
                            if not (isinstance(i, int) and j < 2):
                                from_shift(dve, 2 * T + j - 2, j - 2, q, y)
                    norm(0, 0)
                    norm(1, 1)
                    dve.wait_ge(c_in, 48)
                    pair_loop(dve, body, first=2, last=True)
                    linear(T - 1, 1)
                    add(T - 1, 1)
                    from_shift(dve, 3 * T - 2, T - 2, 0, y)
                    from_shift(dve, 3 * T - 1, T - 1, 1, y, TAIL)
                    bn_finish(dve, 2)

                @block.tensor
                def _(pe):
                    def turn_x(j, q):
                        pe.wait_ge(xb_ready, j + 1)
                        wait(pe, tr_out, j)
                        for k in range(KT):
                            t = pe.transpose(etp_view()[:, k, :], xb[q][:, k * 128:(k + 1) * 128], idt[0:P, 0:P])
                        t.then_inc(tr, 1)

                    def mul_first(j, q):
                        pe.wait_ge(tr_out, j + 1)
                        wait(pe, yc_ready, j - 1)
                        for h in range(H3):
                            t = pe.matmul(pj1_of[q][0:P, h * D3:(h + 1) * D3], xt[q][:, h, :], wt_sb[:, h, :],
                                          start=True, stop=True)
                        t.then_inc(mm1_done, 1)

                    def turn_y(j, q):
                        pe.wait_ge(yc_ready, j + 1)
                        wait(pe, tr1_out, j)
                        for k in range(KT):
                            t = pe.transpose(tp1_view()[:, k, :], yc[q][:, k * 128:(k + 1) * 128], idt[0:P, 0:P])
                        t.then_inc(tr1, 1)

                    def mul(j, q):
                        pe.wait_ge(tr1_out, j + 1)
                        wait(pe, z_ready, j - 1)
                        for k in range(KT):
                            t = pe.matmul(pj_of[q][0:P, :], yt[q][:, k, :], w_sb[:, k, :], start=(k == 0),
                                          stop=(k == KT - 1))
                        t.then_inc(mm_done, 1)

                    def body(i):
                        for q in (0, 1):
                            j = 2 * i + q
                            before = not (isinstance(i, int) and j == 0)
                            ahead = not (isinstance(i, int) and j + 1 >= T)
                            if before:
                                turn_y(j - 1, 1 - q)
                            if ahead:
                                turn_x(j + 1, 1 - q)
                            if isinstance(i, int) and j == 2:
                                shift_matmul(pe, 2, HA[0:P, 0, 0:D])
                            if before:
                                mul(j - 1, 1 - q)
                            if ahead:
                                mul_first(j + 1, 1 - q)
                    turn_x(0, 0)
                    pe.wait_ge(c_in, 48)
                    mul_first(0, 0)
                    pair_loop(pe, body, first=2, last=True)
                    turn_y(T - 1, 1)
                    mul(T - 1, 1)
                    bn_total(pe, 2)

                @block.scalar
                def _(act):
                    def copy_x(j, q):
                        act.wait_ge(tr, j + 1)
                        wait(act, mm1_done, j - 1)
                        act.activation(xt[q][:, :, :], etp_view(), ACT.Copy).then_inc(tr_out, 1)

                    def first_expo(j, q):
                        act.wait_ge(mm1_done, j + 1)
                        wait(act, u1_ready, j - 1)
                        act.activation(e1[q][:, :], pj1_of[q][0:P, :], ACT.Exp).then_inc(e1_ready, 1)

                    def copy_y(j, q):
                        act.wait_ge(tr1, j + 1)
                        wait(act, mm_done, j - 1)
                        act.activation(yt[q][:, :, :], tp1_view(), ACT.Copy).then_inc(tr1_out, 1)

                    def expo(j, q):
                        act.wait_ge(z_ready, j + 1)
                        wait(act, u_ready, j - 1)
                        act.activation(e[q][:, :], z[q][:, :], ACT.Exp).then_inc(e_ready, 1)

                    def body(i):
                        for q in (0, 1):
                            j = 2 * i + q
                            before = not (isinstance(i, int) and j == 0)
                            first_expo(j, q)
                            if before:
                                copy_y(j - 1, 1 - q)
                            if not (isinstance(i, int) and j + 1 >= T):
                                copy_x(j + 1, 1 - q)
                            if not (isinstance(i, int) and j < 3):
                                square(act, 2 * T + j - 3, 1 - q, y, ysq)
                            if before:
                                expo(j - 1, 1 - q)
                    copy_x(0, 0)
                    pair_loop(act, body, first=2, last=True)
                    copy_y(T - 1, 1)
                    square(act, 3 * T - 3, 1, y, ysq)
                    expo(T - 1, 1)
                    square(act, 3 * T - 2, 0, y, ysq)
                    square(act, 3 * T - 1, 1, y, ysq, TAIL)

                @block.gpsimd
                def _(pool):
                    sums_clear(pool, 2)
                    sums_loop(pool, 2 * T, y, ysq)
                    bn_power(pool, 2)
        dec.close()

        with ExitStack() as ph:
            R, xn, st, xin, xt, bias, w_sb = norm_buffers(ph)
            xa = [sb(ph, f"xa{q}", [P, D]) for q in (0, 1)]
            m_in = sems("last_x_in")
            xa_ready = sem("last_xa")
            with nc.Block() as block:
                @block.sync
                def _(sp):
                    def body(i):
                        for q in (0, 1):
                            j = 2 * i + q
                            wait(sp, r_full, 3 * T + j - 1)
                            sp.dma_start(xin[q][:, :], xs[2][j]).then_inc(m_in[q], 16)
                    pair_loop(sp, body, first=True)

                @block.vector
                def _(dve):
                    def body(i):
                        for q in (0, 1):
                            j = 2 * i + q
                            n = 3 * T + j
                            dve.wait_ge(xa_ready, j + 1)
                            dve.tensor_tensor(R[q][:, :], xa[q][:, :], a_bn[1][:, :], ALU.add).then_inc(r_half, 1)
                            dve.wait_ge(r_half, 2 * T + j + 1)
                            dve.wait_ge(m_in[q], 16 * (i + 1))
                            dve.tensor_tensor(R[q][:, :], R[q][:, :], xin[q][:, :], ALU.add).then_inc(r_full, 1)
                            ln_tile(dve, n, q, R, st, xn)
                            dve.wait_ge(xn_stored[q], 16 * (3 * PAIRS + i))
                            ln_write(dve, n, q, R, st, xn[q][:, :])
                    pair_loop(dve, body)

                @block.gpsimd
                def _(pool):
                    def scaled(j, q):
                        wait(pool, r_half, 2 * T + j - 1)
                        pool.tensor_tensor(xa[q][:, :], HA[0:P, j, 0:D], a_bn[0][:, :], ALU.mult).then_inc(xa_ready, 1)

                    def body(i):
                        for q in (0, 1):
                            j = 2 * i + q
                            if not (isinstance(i, int) and j + 1 >= T):
                                scaled(j + 1, 1 - q)
                            norm_store(pool, i, q, 3 * T + j, out, st, xn)
                    scaled(0, 0)
                    pair_loop(pool, body, last=True)
                    for q in (0, 1):
                        pool.wait_ge(xn_stored[q], 16 * 4 * PAIRS)




def _p(a):
    import numpy as np
    return np.pad(a, [(0, NP - N if s == N else 0) for s in a.shape])


def layout(inputs):
    import numpy as np
    g = {k: np.asarray(v) for k, v in inputs.items()}

    def blocks(w):
        return np.ascontiguousarray(w.reshape(KT, 128, -1).transpose(1, 0, 2))

    def columns(v):
        return np.ascontiguousarray(v.reshape(KT, 128).T)

    adj = _p(g["adj"])
    adj_t = np.ascontiguousarray(adj.T)
    L3 = "L3_gnn_"
    return {
        "x": _p(g["x"]).reshape(T, P, D),
        "adj_rows": adj.reshape(T, P, NP),
        "adj_cols": adj_t.reshape(T, P, NP),
        "adj_tiles": np.ascontiguousarray(adj.reshape(T, P, T, P).transpose(0, 3, 2, 1)),
        "ident": np.eye(128, dtype=np.float32),
        "w0": blocks(g["L0_gnn_kernels"].transpose(1, 0, 2).reshape(D, D)),
        "a0_self": g["L0_gnn_attn_self"].reshape(D),
        "a0_neigh": g["L0_gnn_attn_neigh"].reshape(D),
        "b0": g["L0_gnn_biases"].reshape(D),
        "w1": blocks(g["L1_gnn_W"].transpose(1, 0, 2).reshape(D, D)),
        "b1": g["L1_gnn_b"].reshape(D),
        "w2a": blocks(g["L2_gnn_W"][:D]),
        "w2b": blocks(g["L2_gnn_W"][D:]),
        "a2_w": g["L2_gnn_a_w"],
        "a2_b": g["L2_gnn_a_b"].reshape(1),
        "fc_w": blocks(g["L2_gnn_fc_w"]),
        "fc_b": g["L2_gnn_fc_b"],
        "w3": np.ascontiguousarray(g[L3 + "W"].transpose(1, 0, 2)).reshape(D3, D),
        "w3t": np.ascontiguousarray(g[L3 + "W"].transpose(2, 0, 1)).reshape(D3, D),
        "v3a": np.ascontiguousarray(g[L3 + "V"][:, 0, :, 0]).reshape(D),
        "v3b": np.ascontiguousarray(g[L3 + "V"][:, 1, :, 0]).reshape(D),
        "enc_w": blocks(g[L3 + "enc_mlp_W"].T),
        "enc_b": g[L3 + "enc_mlp_b"],
        "dec_w": blocks(g[L3 + "dec_mlp_W"].T),
        "dec_b": g[L3 + "dec_mlp_b"],
        "g_bn": np.stack([columns(g[L3 + k]) for k in ("enc_bn_gamma", "enc_mlp_bn_gamma", "dec_mlp_bn_gamma")], 1),
        "b_bn": np.stack([columns(g[L3 + k]) for k in ("enc_bn_beta", "enc_mlp_bn_beta", "dec_mlp_bn_beta")], 1),
    }


def kernel(**inputs):
    import numpy as _np
    import concourse.bacc as _bacc
    from concourse import mybir as _mybir
    from concourse.bass_utils import run_bass_kernel_spmd as _run

    nc = _bacc.Bacc("TRN2", target_bir_lowering=False, num_devices=1)
    arrays = layout(inputs)
    aps = {k: nc.dram_tensor(f"in_{k}", a.shape, _mybir.dt.from_np(a.dtype), kind="ExternalInput").ap()
           for k, a in arrays.items()}
    out = nc.dram_tensor("out_0", (T, P, D), _mybir.dt.float32, kind="ExternalOutput").ap()
    build(nc, **aps, out=out)
    r = _run(nc, [{f"in_{k}": a for k, a in arrays.items()}], core_ids=[0])
    return _np.ascontiguousarray(r.results[0]["out_0"].reshape(NP, D)[:N])
```
